# Optimizing a Trainium2 kernel written in Bass

```python
import numpy as np
import jax
import jax.numpy as jnp

def _softmax(x, axis=-1):
    return jax.nn.softmax(x, axis=axis)

def _gelu(x):
    return jax.nn.gelu(x, approximate=True)

def _silu(x):
    return jax.nn.silu(x)

def _sigmoid(x):
    return jax.nn.sigmoid(x)

def _layernorm(x, axis=-1, eps=1e-05):
    m = jnp.mean(x, axis=axis, keepdims=True)
    v = jnp.var(x, axis=axis, keepdims=True)
    return (x - m) / jnp.sqrt(v + eps)

def _scatter_add(tgt, idx, src, axis=0):
    return tgt.at[idx].add(src)

def _segment_sum(src, seg, n):
    return jax.ops.segment_sum(src, seg, n)
kernel_name = 'mk_flamingo_gated_d1_seqx_r4_c527e0'

def setup_inputs(seed: int=0):
    np.random.seed(seed)
    _w = jnp.asarray

    def _rec_inputs():
        import jax
        import jax.numpy as jnp
        _rk = jax.random.key(seed)
        x = 0.002226 + 0.9996 * jax.random.normal(jax.random.fold_in(_rk, 1), (8, 112, 256), jnp.float32)
        _lenS = 112 - jax.random.randint(jax.random.fold_in(_rk, 7), (8,), 0, max(1, 112 // 4) + 1, jnp.int32)
        _lenS2 = 375 - jax.random.randint(jax.random.fold_in(_rk, 8), (8,), 0, max(1, 375 // 4) + 1, jnp.int32)
        _ctx_1024P = jax.random.normal(jax.random.fold_in(_rk, 11), (8, 16, 256), jnp.float32)
        _ctx_1024c = jax.random.dirichlet(jax.random.fold_in(_rk, 511), 0.3 * jnp.ones((16,), jnp.float32), (8, 375))
        _ctx_1024t = jnp.einsum('bsk,bkd->bsd', _ctx_1024c, _ctx_1024P)
        _ctx_1024t = _ctx_1024t * jax.lax.rsqrt(jnp.mean(jnp.square(_ctx_1024t)) + 1e-12) * 0.953939
        ctx_1024 = -7.10856e-05 + 0.999911 * (_ctx_1024t + 0.3 * jax.random.normal(jax.random.fold_in(_rk, 611), (8, 375, 256), jnp.float32))
        _g = jax.random.normal(jax.random.fold_in(_rk, 9001), (2, 1), jnp.float32)
        _g = jnp.sign(_g) * jnp.maximum(jnp.abs(_g), 1.0) + (_g == 0) * 1.0
        g_xattn = _g[0]
        g_ffn = _g[1]
        return (x, ctx_1024, g_xattn, g_ffn)
    x, ctx_1024, g_xattn, g_ffn = _rec_inputs()

    def _L0_xattn_setup():
        import jax, jax.numpy as jnp
        import numpy as np
        DIM = 256
        HEAD_DIM = 64
        NUM_HEADS = 8
        INNER = HEAD_DIM * NUM_HEADS
        ROT_DIM = HEAD_DIM
        ROPE_BASE = 10000.0
        EPS = 1e-05

        def layer_norm(x, g, b):
            mu = jnp.mean(x, axis=-1, keepdims=True)
            var = jnp.var(x, axis=-1, keepdims=True)
            return (x - mu) * jax.lax.rsqrt(var + EPS) * g + b

        def rope_rotate_k(k):
            n = k.shape[1]
            half = ROT_DIM // 2
            inv_freq = 1.0 / ROPE_BASE ** (jnp.arange(0, ROT_DIM, 2, dtype=jnp.float32) / ROT_DIM)
            theta = jnp.arange(n, dtype=jnp.float32)[:, None] * inv_freq[None, :]
            angles = jnp.concatenate([theta, theta], axis=-1)
            cos = jnp.cos(angles)[None, :, None, :].astype(k.dtype)
            sin = jnp.sin(angles)[None, :, None, :].astype(k.dtype)
            k_rope, k_pass = (k[..., :ROT_DIM], k[..., ROT_DIM:])
            neg_half = jnp.concatenate([-k_rope[..., half:], k_rope[..., :half]], axis=-1)
            k_rope = k_rope * cos + neg_half * sin
            return jnp.concatenate([k_rope, k_pass], axis=-1)
        key = jax.random.key(seed)
        ks = jax.random.split(key, 5)
        b, n, m = (8, 2048, 64)
        s = 1.0 / np.sqrt(DIM)
        return {'x': jax.random.normal(ks[0], (b, n, DIM), jnp.float32), 'latents': jax.random.normal(ks[1], (b, m, DIM), jnp.float32), 'gamma_x': jnp.ones((DIM,), jnp.float32), 'beta_x': jnp.zeros((DIM,), jnp.float32), 'gamma_l': jnp.ones((DIM,), jnp.float32), 'beta_l': jnp.zeros((DIM,), jnp.float32), 'Wq': jax.random.normal(ks[2], (DIM, INNER), jnp.float32) * s, 'Wkv': jax.random.normal(ks[3], (DIM, 2 * INNER), jnp.float32) * s, 'Wo': jax.random.normal(ks[4], (INNER, DIM), jnp.float32) * (1.0 / np.sqrt(INNER))}
    _L0_xattn_all = _L0_xattn_setup()
    _L0_xattn_in = {k: v for k, v in _L0_xattn_all.items() if k in ('gamma_x', 'beta_x', 'gamma_l', 'beta_l', 'Wq', 'Wkv', 'Wo')}
    del _L0_xattn_all

    def _L0_ffn_setup():
        import jax, jax.numpy as jnp
        import numpy as np
        B, S, D = (4, 512, 256)
        F = 1024
        E = 8
        K = 2
        EPS = 1e-09
        key = jax.random.key(seed)
        ks = jax.random.split(key, 6)
        scale = 0.02
        return {'x': jax.random.normal(ks[0], (B, S, D), dtype=jnp.float32), 'Wg': jax.random.normal(ks[1], (D, E), dtype=jnp.float32) * scale, 'W1': jax.random.normal(ks[2], (E, D, F), dtype=jnp.float32) * scale, 'b1': jnp.zeros((E, F), dtype=jnp.float32), 'W2': jax.random.normal(ks[3], (E, F, D), dtype=jnp.float32) * scale, 'b2': jnp.zeros((E, D), dtype=jnp.float32)}
    _L0_ffn_all = _L0_ffn_setup()
    _L0_ffn_in = {k: v for k, v in _L0_ffn_all.items() if k in ('Wg', 'W1', 'b1', 'W2', 'b2')}
    del _L0_ffn_all
    return {'x': x, 'ctx_1024': ctx_1024, 'g_xattn': g_xattn, 'g_ffn': g_ffn, 'L0_xattn_gamma_x': _L0_xattn_in['gamma_x'], 'L0_xattn_beta_x': _L0_xattn_in['beta_x'], 'L0_xattn_gamma_l': _L0_xattn_in['gamma_l'], 'L0_xattn_beta_l': _L0_xattn_in['beta_l'], 'L0_xattn_Wq': _L0_xattn_in['Wq'], 'L0_xattn_Wkv': _L0_xattn_in['Wkv'], 'L0_xattn_Wo': _L0_xattn_in['Wo'], 'L0_ffn_Wg': _L0_ffn_in['Wg'], 'L0_ffn_W1': _L0_ffn_in['W1'], 'L0_ffn_b1': _L0_ffn_in['b1'], 'L0_ffn_W2': _L0_ffn_in['W2'], 'L0_ffn_b2': _L0_ffn_in['b2']}

def reference(x, ctx_1024, g_xattn, g_ffn, L0_xattn_gamma_x, L0_xattn_beta_x, L0_xattn_gamma_l, L0_xattn_beta_l, L0_xattn_Wq, L0_xattn_Wkv, L0_xattn_Wo, L0_ffn_Wg, L0_ffn_W1, L0_ffn_b1, L0_ffn_W2, L0_ffn_b2):
    import jax
    import jax.numpy as jnp

    def _L0_xattn_ref(x, latents, gamma_x, beta_x, gamma_l, beta_l, Wq, Wkv, Wo):
        import jax, jax.numpy as jnp
        import numpy as np
        DIM = 256
        HEAD_DIM = 64
        NUM_HEADS = 8
        INNER = HEAD_DIM * NUM_HEADS
        ROT_DIM = HEAD_DIM
        ROPE_BASE = 10000.0
        EPS = 1e-05

        def layer_norm(x, g, b):
            mu = jnp.mean(x, axis=-1, keepdims=True)
            var = jnp.var(x, axis=-1, keepdims=True)
            return (x - mu) * jax.lax.rsqrt(var + EPS) * g + b

        def rope_rotate_k(k):
            n = k.shape[1]
            half = ROT_DIM // 2
            inv_freq = 1.0 / ROPE_BASE ** (jnp.arange(0, ROT_DIM, 2, dtype=jnp.float32) / ROT_DIM)
            theta = jnp.arange(n, dtype=jnp.float32)[:, None] * inv_freq[None, :]
            angles = jnp.concatenate([theta, theta], axis=-1)
            cos = jnp.cos(angles)[None, :, None, :].astype(k.dtype)
            sin = jnp.sin(angles)[None, :, None, :].astype(k.dtype)
            k_rope, k_pass = (k[..., :ROT_DIM], k[..., ROT_DIM:])
            neg_half = jnp.concatenate([-k_rope[..., half:], k_rope[..., :half]], axis=-1)
            k_rope = k_rope * cos + neg_half * sin
            return jnp.concatenate([k_rope, k_pass], axis=-1)
        b, n, _ = x.shape
        m = latents.shape[1]
        h, d = (NUM_HEADS, HEAD_DIM)
        scale = d ** (-0.5)
        xn = layer_norm(x, gamma_x, beta_x)
        ln = layer_norm(latents, gamma_l, beta_l)
        q = (ln @ Wq).reshape(b, m, h, d)
        kv_x = xn @ Wkv
        k_x, v_x = (kv_x[..., :INNER], kv_x[..., INNER:])
        kv_l = ln @ Wkv
        k_l, v_l = (kv_l[..., :INNER], kv_l[..., INNER:])
        k_x = k_x.reshape(b, n, h, d)
        v_x = v_x.reshape(b, n, h, d)
        k_x = rope_rotate_k(k_x)
        q = jnp.transpose(q, (0, 2, 1, 3)) * scale
        k_x = jnp.transpose(k_x, (0, 2, 1, 3))
        v_x = jnp.transpose(v_x, (0, 2, 1, 3))
        k_l = jnp.transpose(k_l.reshape(b, m, h, d), (0, 2, 1, 3))
        v_l = jnp.transpose(v_l.reshape(b, m, h, d), (0, 2, 1, 3))
        k = jnp.concatenate([k_x, k_l], axis=2)
        v = jnp.concatenate([v_x, v_l], axis=2)
        sim = jnp.einsum('bhid,bhjd->bhij', q, k)
        attn = jax.nn.softmax(sim, axis=-1)
        out = jnp.einsum('bhij,bhjd->bhid', attn, v)
        out = jnp.transpose(out, (0, 2, 1, 3)).reshape(b, m, INNER)
        return out @ Wo

    def _L0_ffn_ref(x, Wg, W1, b1, W2, b2):
        import jax, jax.numpy as jnp
        import numpy as np
        B, S, D = (4, 512, 256)
        F = 1024
        E = 8
        K = 2
        EPS = 1e-09
        logits = jnp.einsum('bsd,de->bse', x, Wg)
        P = jax.nn.softmax(logits, axis=-1)
        _, topk_idx = jax.lax.top_k(P, K)
        mask = jax.nn.one_hot(topk_idx, E, dtype=x.dtype).sum(-2)
        P_topk = P * mask
        P_norm = P_topk / (P_topk.sum(axis=-1, keepdims=True) + EPS)
        h = jax.nn.gelu(jnp.einsum('bsd,edf->ebsf', x, W1) + b1[:, None, None, :], approximate=False)
        y_e = jnp.einsum('ebsf,efd->ebsd', h, W2) + b2[:, None, None, :]
        y = jnp.einsum('ebsd,bse->bsd', y_e, P_norm)
        return y
    x = x + jnp.tanh(g_xattn[0]) * _L0_xattn_ref(ctx_1024, _layernorm(x, axis=-1), L0_xattn_gamma_x, L0_xattn_beta_x, L0_xattn_gamma_l, L0_xattn_beta_l, L0_xattn_Wq, L0_xattn_Wkv, L0_xattn_Wo)
    x = x + jnp.tanh(g_ffn[0]) * _L0_ffn_ref(_layernorm(x, axis=-1), L0_ffn_Wg, L0_ffn_W1, L0_ffn_b1, L0_ffn_W2, L0_ffn_b2)
    return x

_drawn_inputs = setup_inputs


def setup_inputs(seed=0):
    import zlib

    import numpy as np

    out = dict(_drawn_inputs(seed))
    spreads = {'L0_xattn_gamma_x': (1.0, 0.2),
     'L0_xattn_beta_x': (0.0, 0.1),
     'L0_xattn_gamma_l': (1.0, 0.578),
     'L0_xattn_beta_l': (0.0, 0.271),
     'L0_ffn_b1': (0.0, 0.337),
     'L0_ffn_b2': (0.0, 0.1)}
    factors = {}
    for name, (base, spread) in spreads.items():
        noise = np.random.default_rng([zlib.crc32(name.encode()), seed]).standard_normal(out[name].shape)
        drawn = base * np.exp(spread * noise) if base else spread * noise
        out[name] = jnp.asarray(drawn.astype(out[name].dtype))
    for name, factor in factors.items():
        out[name] = (out[name] * factor).astype(out[name].dtype)
    return out
```

```python
from contextlib import ExitStack

import concourse.bass as bass
from concourse import mybir
from concourse.alu_op_type import AluOpType as ALU

F32 = mybir.dt.float32
F32R = mybir.dt.float32r
ACT = mybir.ActivationFunctionType
AX = mybir.AxisListType.X

B, M, D = 8, 112, 256
J = 375
H, DH = 8, 64
INNER = H * DH
E, FF = 8, 1024
P = 128
KD = D // P
JT, JR = 3, J // 3
NT = JT + 1
JA = J + M
JP = JA + 1
PP = NT * JR
HP = H // 2
TOK = B * M
HALF = TOK // 2
FB = FF // P
SCALE = DH ** -0.5
EPS = 1e-5
TOP_EPS = 1e-9
BIG = 4.0


class Tally:

    def __init__(self, sem, per):
        self.sem, self.per = sem, per

    def start(self, eng):
        eng.sem_inc(self.sem, self.per + 1)

    def at(self, t, p, n):
        return t * (2 * self.per) + (self.per * (p + 1) + 1 + n)


def build_program(nc, x, ctx, g_xattn, g_ffn, gamma_x, beta_x, gamma_l, beta_l, wq, wkv, wo,
                  wg, w1, b1, w2, b2, rope, out):
    probs_dram = nc.dram_tensor("probs_scratch", [E, TOK], F32).ap()
    with ExitStack() as whole:
        def keep(name, shape, dt=F32):
            return whole.enter_context(nc.sbuf_tensor(name, shape, dt))

        x_all = keep("x_all", [M, B, D])
        ident = keep("ident", [P, P])
        gates = keep("gates", [P, 2])
        neg_half = keep("neg_half", [P, B])
        w1s = keep("w1s", [P, KD, FF])
        w2s = keep("w2s", [P, FB, D])
        w1_loaded = whole.enter_context(nc.semaphore("w1_loaded"))
        w2_loaded = whole.enter_context(nc.semaphore("w2_loaded"))
        attention(nc, x, ctx, g_xattn, g_ffn, gamma_x, beta_x, gamma_l, beta_l, wq, wkv, wo, rope,
                  x_all, ident, gates, neg_half, w1s, w2s)
        experts(nc, wg, w1, b1, w2, b2, out, probs_dram, x_all, ident, gates, neg_half, w1s, w2s,
                w1_loaded, w2_loaded)


def attention(nc, x, ctx, g_xattn, g_ffn, gamma_x, beta_x, gamma_l, beta_l, wq, wkv, wo, rope,
              x_all, ident, gates, neg_half, w1s, w2s):
    with ExitStack() as st:
        def sb(name, shape, dt=F32):
            return st.enter_context(nc.sbuf_tensor(name, shape, dt))

        def ps(name):
            return st.enter_context(nc.psum_tensor(name, [P, 512], F32))

        def sem(name):
            return st.enter_context(nc.semaphore(name))

        def tally(name, per):
            return Tally(sem(name), per)

        wkvh, wkvl = sb("wkvh", [P, KD, 2 * INNER], F32R), sb("wkvl", [P, KD, 2 * INNER], F32R)
        wqh, wql = sb("wqh", [P, KD, INNER], F32R), sb("wql", [P, KD, INNER], F32R)
        woh, wol = sb("woh", [P, HP, D], F32R), sb("wol", [P, HP, D], F32R)
        affine_rows = sb("affine_rows", [4 * KD, P])
        affine = sb("affine", [P, 4, KD])
        rope_t = sb("rope_t", [JR, 2, JT, DH])
        krot = sb("krot", [JR, 2, 2, INNER])
        kcos, ksin = krot[:, 0], krot[:, 1]
        xn = krot[0:M].rearrange("q a s (c d) -> q (a s c) d", d=D)
        lstat, lmv = sb("lstat", [M, B, 6]), sb("lmv", [M, B, 2])
        lvar, lrstd = sb("lvar", [M, B]), sb("lrstd", [M, B])
        lf = sb("lf", [P, 2, KD, M])
        lnh, lnl = sb("lnh", [P, KD, TOK], F32R), sb("lnl", [P, KD, TOK], F32R)
        lath, latl = sb("lath", [P, 2, KD, M], F32R), sb("latl", [P, 2, KD, M], F32R)
        qh, ql = sb("qh", [P, 2, HP, M], F32R), sb("ql", [P, 2, HP, M], F32R)
        ctx_t = sb("ctx_t", [JR, 2, JT, D])
        cstat = sb("cstat", [JR, JT, 6])
        csum, cdiff, csq, cmean = (sb(n, [JR, JT]) for n in ("csum", "cdiff", "csq", "cmean"))
        cvar, crstd = sb("cvar", [JR, JT]), sb("crstd", [JR, JT])
        cf = sb("cf", [P, JT, KD, JR])
        ch, cl = sb("ch", [P, JT, KD, JR], F32R), sb("cl", [P, JT, KD, JR], F32R)
        krow = sb("krow", [JR, NT, INNER])
        kth, ktl = sb("kth", [P, 2, HP, JP], F32R), sb("ktl", [P, 2, HP, JP], F32R)
        vh, vl = sb("vh", [JR, 2, NT, INNER], F32R), sb("vl", [JR, 2, NT, INNER], F32R)
        negmax, total, inv = sb("negmax", [M, 2]), sb("total", [M, 2]), sb("inv", [M, 2])
        prob = sb("prob", [M, 2, PP])
        pth, ptl = sb("pth", [JR, 2, NT, 2, M], F32R), sb("ptl", [JR, 2, NT, 2, M], F32R)
        oth, otl = sb("oth", [P, HP, M], F32R), sb("otl", [P, HP, M], F32R)
        tp, pk, pv, po = ps("tp"), ps("pk"), ps("pv"), ps("po")
        sc = [ps("sc0"), ps("sc1")]
        pt = [ps("pt0"), ps("pt1")]

        x_loaded, w_loaded, small_loaded = sem("x_loaded"), sem("w_loaded"), sem("small_loaded")
        wqo_loaded = sem("wqo_loaded")
        ident_set, const_set, pad_set = sem("ident_set"), sem("const_set"), sem("pad_set")
        tanh_done = sem("tanh_done")
        affine_tr, affine_done = sem("affine_tr"), sem("affine_done")
        whi_done, wlo_done = sem("whi_done"), sem("wlo_done")
        lstat_done, lmv_done, lvar_done, lrstd_done, lnorm_done = (
            sem("lstat_done"), sem("lmv_done"), sem("lvar_done"), sem("lrstd_done"), sem("lnorm_done"))
        ltr_done, lf_done, lnh_done, lnl_done = sem("ltr_done"), sem("lf_done"), sem("lnh_done"), sem("lnl_done")
        ctx_loaded = [sem("ctx_loaded0"), sem("ctx_loaded1")]
        cstat_done, cparts_done, cvar_done = tally("cstat_done", JT), tally("cparts_done", 3), tally("cvar_done", 2)
        crstd_done, cnorm_done = tally("crstd_done", 1), tally("cnorm_done", JT)
        ctr_done, cf_done = tally("ctr_done", JT), tally("cf_done", JT)
        ch_done, cl_done = tally("ch_done", JT), tally("cl_done", JT)
        lat_ready, qproj_done = tally("lat_ready", 1), tally("qproj_done", 1)
        qh_done, ql_done = tally("qh_done", 1), tally("ql_done", 1)
        kproj_done, vproj_done = tally("kproj_done", NT), tally("vproj_done", NT)
        rope_done, krow_done, klat_done = tally("rope_done", JT), tally("krow_done", JT), tally("klat_done", 1)
        ktr_done, kth_done, ktl_done = tally("ktr_done", NT), tally("kth_done", NT), tally("ktl_done", NT)
        vh_done, vl_done = tally("vh_done", NT), tally("vl_done", NT)
        score_done, max_done, exp_done = tally("score_done", H), tally("max_done", H), tally("exp_done", H)
        inv_done, prob_done = tally("inv_done", H), tally("prob_done", H)
        ptr_done, pth_done, ptl_done = tally("ptr_done", H), tally("pth_done", H), tally("ptl_done", H)
        av_done, oth_done, otl_done = tally("av_done", HP), tally("oth_done", HP), tally("otl_done", HP)
        wo_done, x1_done = tally("wo_done", 1), tally("x1_done", 1)

        block = st.enter_context(nc.Block())

        ORDER = [JT, 0, 1, 2]

        @block.sync
        def _(sp):
            sp.dma_start(x_all[:], x.rearrange("b m d -> m b d")).then_inc(x_loaded, 16)
            sp.dma_start(w1s[:, :, :], wkv.rearrange("(k p) n -> p k n", p=P)).then_inc(w_loaded, 16)
            sp.dma_start(w2s[:, 0:4, :].rearrange("p (k a) d -> p k (a d)", k=KD),
                         wq.rearrange("(k p) n -> p k n", p=P)).then_inc(wqo_loaded, 16)
            sp.dma_start(w2s[:, 4:8, :], wo.rearrange("(k p) n -> p k n", p=P)).then_inc(wqo_loaded, 16)
            with sp.Fori(0, B // 2) as t:
                for p in range(2):
                    sp.wait_ge(ctr_done.sem, ctr_done.at(t, p, -JT))
                    sp.dma_start(ctx_t[:, p], ctx[2 * t + p].rearrange("(a r) d -> r a d", a=JT)) \
                        .then_inc(ctx_loaded[p], 16)

        @block.gpsimd
        def _(pool):
            for c in (crstd_done, cl_done, krow_done):
                c.start(pool)
            pool.dma_start(rope_t[:], rope).then_inc(small_loaded, 16)
            for n, v in enumerate((gamma_x, beta_x, gamma_l, beta_l)):
                pool.dma_start(affine_rows[n * KD:(n + 1) * KD, :], v.rearrange("(k p) -> k p", p=P)).then_inc(small_loaded, 16)
            pool.dma_start(gates[:, 0:1], g_xattn.rearrange("(a b) -> a b", b=1).broadcast_to([P, 1])) \
                .then_inc(small_loaded, 16)
            pool.dma_start(gates[:, 1:2], g_ffn.rearrange("(a b) -> a b", b=1).broadcast_to([P, 1])) \
                .then_inc(small_loaded, 16)
            pool.memset(ident[:], 0.0).then_inc(const_set, 1)
            pool.memset(neg_half[:], -0.5).then_inc(const_set, 1)
            pool.wait_ge(const_set, 2)
            pool.affine_select(out=ident[:], in_=ident[:], compare_op=ALU.not_equal, fill=1.0, base=0,
                               pattern=[[-1, P]], channel_multiplier=1).then_inc(ident_set, 1)
            for r in range(2):
                pool.wait_ge(lmv_done, B * (r + 1))
                pool.tensor_scalar(lvar[:], lmv[:, :, 1], EPS, None, ALU.add).then_inc(lvar_done, 1)
                pool.wait_ge(lvar_done, r + 1)
                pool.tensor_tensor(lrstd[:], lvar[:], neg_half[0:M, :], ALU.pow).then_inc(lrstd_done, 1)
            for b in range(B):
                pool.wait_ge(lnh_done, b + 1)
                pool.tensor_tensor(lnl[:, :, b * M:(b + 1) * M], lf[:, b % 2],
                                   lnh[:, :, b * M:(b + 1) * M].bitcast(F32), ALU.subtract).then_inc(lnl_done, 1)
            with pool.Fori(0, B // 2) as t:
                for p in range(2):
                    pool.wait_ge(cvar_done.sem, cvar_done.at(t, p, 2))
                    pool.tensor_tensor(crstd[:], cvar[:], neg_half[0:JR, 0:JT], ALU.pow).then_inc(crstd_done.sem, 1)

                    def low_context(j):
                        pool.wait_ge(ch_done.sem, ch_done.at(t, p, j + 1))
                        pool.tensor_tensor(cl[:, j], cf[:, j], ch[:, j].bitcast(F32), ALU.subtract) \
                            .then_inc(cl_done.sem, 1)

                    def rotated(j):
                        pool.wait_ge(rope_done.sem, rope_done.at(t, p, j + 1))
                        pool.wait_ge(ktr_done.sem, ktr_done.at(t, p, j + 2 - NT))
                        pool.tensor_tensor(krow[:, j], kcos[:, j % 2], ksin[:, j % 2], ALU.add) \
                            .then_inc(krow_done.sem, 1)

                    low_context(0)
                    low_context(1)
                    rotated(0)
                    low_context(2)
                    rotated(1)
                    rotated(2)

        @block.scalar
        def _(act):
            for c in (lat_ready, ch_done, qh_done, klat_done, kth_done, vh_done, exp_done, pth_done, oth_done):
                c.start(act)
            act.wait_ge(small_loaded, 7 * 16)
            act.activation(gates[:], gates[:], ACT.Tanh).then_inc(tanh_done, 1)
            act.wait_ge(w_loaded, 16)
            act.copy(wkvh[:], w1s[:]).then_inc(whi_done, 1)
            act.wait_ge(wqo_loaded, 32)
            act.copy(wqh[:].rearrange("p k (a d) -> p (k a) d", d=D), w2s[:, 0:4, :]).then_inc(whi_done, 1)
            act.copy(woh[:], w2s[:, 4:8, :]).then_inc(whi_done, 1)
            for b in range(B):
                act.wait_ge(lf_done, b + 1)
                act.copy(lnh[:, :, b * M:(b + 1) * M], lf[:, b % 2]).then_inc(lnh_done, 1)
            act.wait_ge(lnh_done, B)
            act.wait_ge(lnl_done, B)
            with act.Fori(0, B // 2) as t:
                for p in range(2):
                    def high_context(j):
                        act.wait_ge(cf_done.sem, cf_done.at(t, p, j + 1))
                        act.wait_ge(vproj_done.sem, vproj_done.at(t, p, j + 2 - NT))
                        act.copy(ch[:, j], cf[:, j]).then_inc(ch_done.sem, 1)

                    def high_value(n):
                        j = ORDER[n]
                        rows = M if j == JT else JR
                        act.wait_ge(vproj_done.sem, vproj_done.at(t, p, n + 1))
                        act.wait_ge(av_done.sem, av_done.at(t, p, -HP))
                        act.copy(vh[0:rows, p, j], pv[0:rows, :]).then_inc(vh_done.sem, 1)

                    def high_key(n):
                        j = ORDER[n]
                        rows = M if j == JT else JR
                        act.wait_ge(ktr_done.sem, ktr_done.at(t, p, n + 1))
                        act.wait_ge(score_done.sem, score_done.at(t, p, -H))
                        act.copy(kth[:, p, :, j * JR:j * JR + rows],
                                 tp[:, 0:HP * P].rearrange("q (a r) -> q a r", a=HP)[:, :, 0:rows]) \
                            .then_inc(kth_done.sem, 1)

                    act.wait_ge(vproj_done.sem, vproj_done.at(t, p, -NT))
                    cols = bass.ds((2 * t + p) * M, M)
                    act.copy(lath[:, p], lnh[:, :, cols].bitcast(F32))
                    act.copy(latl[:, p], lnl[:, :, cols].bitcast(F32)).then_inc(lat_ready.sem, 1)
                    act.wait_ge(qproj_done.sem, qproj_done.at(t, p, 1))
                    act.wait_ge(score_done.sem, score_done.at(t, p, -H))
                    act.activation(qh[:, p], po[:, 0:HP * M].rearrange("q (a r) -> q a r", a=HP), ACT.Copy,
                                   scale=SCALE).then_inc(qh_done.sem, 1)
                    high_context(0)
                    act.wait_ge(kproj_done.sem, kproj_done.at(t, p, 1))
                    act.wait_ge(ktr_done.sem, ktr_done.at(t, p, 1 - NT))
                    act.copy(krow[0:M, JT], pk[0:M, :]).then_inc(klat_done.sem, 1)
                    high_value(0)
                    high_context(1)
                    high_key(0)
                    high_value(1)
                    high_context(2)
                    high_value(2)
                    high_key(1)
                    high_value(3)
                    high_key(2)
                    high_key(3)

                    def exponent(h):
                        act.wait_ge(max_done.sem, max_done.at(t, p, h + 1))
                        act.wait_ge(ptr_done.sem, ptr_done.at(t, p, h - 1))
                        act.activation(prob[:, h % 2, 0:JA], sc[h % 2][0:M, 0:JA], ACT.Exp,
                                       bias=negmax[:, h % 2:h % 2 + 1],
                                       accum_out=total[:, h % 2:h % 2 + 1]).then_inc(exp_done.sem, 1)

                    def high_prob(h):
                        act.wait_ge(ptr_done.sem, ptr_done.at(t, p, h + 1))
                        act.wait_ge(av_done.sem, av_done.at(t, p, h // 2 - 1))
                        act.copy(pth[:, h // 2 % 2, :, h % 2, :],
                                 pt[h % 2][0:JR, 0:NT * M].rearrange("q (a r) -> q a r", a=NT)) \
                            .then_inc(pth_done.sem, 1)

                    def high_out(a):
                        act.wait_ge(av_done.sem, av_done.at(t, p, a + 1))
                        act.wait_ge(wo_done.sem, wo_done.at(t, p, 0))
                        for u in range(2):
                            r = slice(u * DH, (u + 1) * DH)
                            last = act.copy(oth[r, a, :], po[r, u * M:(u + 1) * M])
                        last.then_inc(oth_done.sem, 1)

                    exponent(0)
                    exponent(1)
                    for h in range(H):
                        high_prob(h)
                        if h + 2 < H:
                            exponent(h + 2)
                        if h % 2 == 0 and h >= 2:
                            high_out(h // 2 - 1)
                    high_out(HP - 1)

        @block.vector
        def _(dve):
            for c in (cstat_done, cparts_done, cvar_done, cnorm_done, cf_done, ql_done, rope_done, ktl_done, vl_done,
                      max_done, inv_done, prob_done, ptl_done, otl_done, x1_done):
                c.start(dve)
            for w in (kth, ktl):
                dve.memset(w[:, :, :, JA:JP].bitcast(F32), 0.0).then_inc(pad_set, 1)
            dve.memset(prob[:, :, JA:PP], 0.0).then_inc(pad_set, 1)
            dve.wait_ge(x_loaded, 16)
            for r in range(2):
                src = x_all if r == 0 else xn
                if r:
                    dve.wait_ge(lnorm_done, B)
                for b in range(B):
                    dve.bn_stats(lstat[:, b, :], src[:, b, :]).then_inc(lstat_done, 1)
                for b in range(B):
                    dve.wait_ge(lstat_done, r * B + b + 1)
                    dve.bn_aggr(lmv[:, b, :], lstat[:, b, :]).then_inc(lmv_done, 1)
                dve.wait_ge(lmv_done, B * (r + 1))
                dve.wait_ge(lrstd_done, r + 1)
                for b in range(B):
                    dve.tensor_scalar(xn[:, b, :], src[:, b, :], lmv[:, b, 0:1], lrstd[:, b:b + 1],
                                      ALU.subtract, ALU.mult).then_inc(lnorm_done, 1)
            dve.wait_ge(affine_tr, 1)
            dve.tensor_copy(affine[:].rearrange("q n k -> q (n k)"), pt[0][:, 0:4 * KD]).then_inc(affine_done, 1)
            dve.wait_ge(affine_done, 1)
            for b in range(B):
                dve.wait_ge(ltr_done, b + 1)
                if b >= 2:
                    dve.wait_ge(lnl_done, b - 1)
                for k in range(KD):
                    last = dve.tensor_scalar(lf[:, b % 2, k, :], sc[b % 2][:, k * M:(k + 1) * M],
                                             affine[:, 2, k:k + 1], affine[:, 3, k:k + 1], ALU.mult, ALU.add)
                last.then_inc(lf_done, 1)
            dve.wait_ge(whi_done, 1)
            dve.tensor_tensor(wkvl[:], w1s[:], wkvh[:].bitcast(F32), ALU.subtract).then_inc(wlo_done, 1)
            dve.wait_ge(whi_done, 3)
            dve.tensor_tensor(wql[:].rearrange("p k (a d) -> p (k a) d", d=D), w2s[:, 0:4, :],
                              wqh[:].rearrange("p k (a d) -> p (k a) d", d=D).bitcast(F32),
                              ALU.subtract).then_inc(wlo_done, 1)
            dve.tensor_tensor(wol[:], w2s[:, 4:8, :], woh[:].bitcast(F32), ALU.subtract).then_inc(wlo_done, 1)
            dve.wait_ge(tanh_done, 1)
            with dve.Fori(0, B // 2) as t:
                for p in range(2):
                    dve.wait_ge(ctx_loaded[p], t * 16 + 16)
                    for j in range(JT):
                        dve.bn_stats(cstat[:, j, :], ctx_t[:, p, j, :]).then_inc(cstat_done.sem, 1)
                    dve.wait_ge(cstat_done.sem, cstat_done.at(t, p, JT))
                    dve.tensor_tensor(csum[:], cstat[:, :, 1], cstat[:, :, 4], ALU.add).then_inc(cparts_done.sem, 1)
                    dve.tensor_tensor(cdiff[:], cstat[:, :, 1], cstat[:, :, 4], ALU.subtract) \
                        .then_inc(cparts_done.sem, 1)
                    dve.tensor_tensor(cvar[:], cstat[:, :, 2], cstat[:, :, 5], ALU.add)
                    dve.wait_ge(cparts_done.sem, cparts_done.at(t, p, 2))
                    dve.tensor_tensor(csq[:], cdiff[:], cdiff[:], ALU.mult)
                    dve.tensor_scalar(cmean[:], csum[:], 0.5, None, ALU.mult).then_inc(cparts_done.sem, 1)
                    dve.wait_ge(cparts_done.sem, cparts_done.at(t, p, 3))
                    dve.scalar_tensor_tensor(cvar[:], csq[:], D / 4.0, cvar[:], ALU.mult, ALU.add) \
                        .then_inc(cvar_done.sem, 1)
                    dve.wait_ge(cvar_done.sem, cvar_done.at(t, p, 1))
                    dve.tensor_scalar(cvar[:], cvar[:], 1.0 / D, EPS, ALU.mult, ALU.add).then_inc(cvar_done.sem, 1)
                    dve.wait_ge(crstd_done.sem, crstd_done.at(t, p, 1))
                    for j in range(JT):
                        dve.tensor_scalar(ctx_t[:, p, j, :], ctx_t[:, p, j, :], cmean[:, j:j + 1], crstd[:, j:j + 1],
                                          ALU.subtract, ALU.mult).then_inc(cnorm_done.sem, 1)

                    def full_context(j):
                        dve.wait_ge(ctr_done.sem, ctr_done.at(t, p, j + 1))
                        dve.wait_ge(cl_done.sem, cl_done.at(t, p, j + 1 - JT))
                        for k in range(KD):
                            last = dve.tensor_scalar(cf[:, j, k, :], tp[:, k * JR:(k + 1) * JR],
                                                     affine[:, 0, k:k + 1], affine[:, 1, k:k + 1],
                                                     ALU.mult, ALU.add)
                        last.then_inc(cf_done.sem, 1)

                    def low_value(n):
                        j = ORDER[n]
                        rows = M if j == JT else JR
                        dve.wait_ge(vh_done.sem, vh_done.at(t, p, n + 1))
                        dve.tensor_tensor(vl[0:rows, p, j], pv[0:rows, :], vh[0:rows, p, j].bitcast(F32),
                                          ALU.subtract).then_inc(vl_done.sem, 1)

                    def low_key(n):
                        j = ORDER[n]
                        rows = M if j == JT else JR
                        dve.wait_ge(kth_done.sem, kth_done.at(t, p, n + 1))
                        c = slice(j * JR, j * JR + rows)
                        dve.tensor_tensor(ktl[:, p, :, c],
                                          tp[:, 0:HP * P].rearrange("q (a r) -> q a r", a=HP)[:, :, 0:rows],
                                          kth[:, p, :, c].bitcast(F32), ALU.subtract).then_inc(ktl_done.sem, 1)

                    def rope_parts(j):
                        dve.wait_ge(kproj_done.sem, kproj_done.at(t, p, j + 2))
                        dve.wait_ge(krow_done.sem, krow_done.at(t, p, j - 1 if j else 0))
                        half = DH // 2
                        dve.tensor_tensor(
                            kcos[:, j % 2].rearrange("q (h c) -> q h c", h=H),
                            pk[0:JR, :].rearrange("q (h c) -> q h c", h=H),
                            rope_t[:, 0, j:j + 1, :].broadcast_to([JR, H, DH]), ALU.mult)
                        for s in range(2):
                            last = dve.tensor_tensor(
                                ksin[:, j % 2].rearrange("q (h s c) -> q h s c", h=H, s=2)[:, :, s, :],
                                pk[0:JR, :].rearrange("q (h s c) -> q h s c", h=H, s=2)[:, :, 1 - s, :],
                                rope_t[:, 1, j:j + 1, s * half:(s + 1) * half].broadcast_to([JR, H, half]),
                                ALU.mult)
                        last.then_inc(rope_done.sem, 1)

                    dve.wait_ge(qh_done.sem, qh_done.at(t, p, 1))
                    dve.scalar_tensor_tensor(ql[:, p], po[:, 0:HP * M].rearrange("q (a r) -> q a r", a=HP), SCALE,
                                             qh[:, p].bitcast(F32), ALU.mult, ALU.subtract).then_inc(ql_done.sem, 1)
                    full_context(0)
                    low_value(0)
                    full_context(1)
                    low_key(0)
                    rope_parts(0)
                    low_value(1)
                    full_context(2)
                    rope_parts(1)
                    low_value(2)
                    low_key(1)
                    rope_parts(2)
                    low_value(3)
                    low_key(2)
                    low_key(3)

                    def row_max(h):
                        dve.wait_ge(score_done.sem, score_done.at(t, p, h + 1))
                        dve.tensor_reduce(negmax[:, h % 2:h % 2 + 1], sc[h % 2][0:M, 0:JA], AX, ALU.max,
                                          negate=True).then_inc(max_done.sem, 1)

                    def normalise(h):
                        dve.wait_ge(exp_done.sem, exp_done.at(t, p, h + 1))
                        s = slice(h % 2, h % 2 + 1)
                        dve.reciprocal(inv[:, s], total[:, s]).then_inc(inv_done.sem, 1)
                        dve.wait_ge(inv_done.sem, inv_done.at(t, p, h + 1))
                        dve.tensor_scalar(prob[:, h % 2, 0:JA], prob[:, h % 2, 0:JA], inv[:, s], None,
                                          ALU.mult).then_inc(prob_done.sem, 1)

                    def low_prob(h):
                        dve.wait_ge(pth_done.sem, pth_done.at(t, p, h + 1))
                        s = (slice(None), h // 2 % 2, slice(None), h % 2)
                        dve.tensor_tensor(ptl[s], pt[h % 2][0:JR, 0:NT * M].rearrange("q (a r) -> q a r", a=NT),
                                          pth[s].bitcast(F32), ALU.subtract).then_inc(ptl_done.sem, 1)

                    def low_out(a):
                        dve.wait_ge(oth_done.sem, oth_done.at(t, p, a + 1))
                        for u in range(2):
                            r = slice(u * DH, (u + 1) * DH)
                            last = dve.tensor_tensor(otl[r, a, :], po[r, u * M:(u + 1) * M],
                                                     oth[r, a, :].bitcast(F32), ALU.subtract)
                        last.then_inc(otl_done.sem, 1)

                    row_max(0)
                    row_max(1)
                    for h in range(H):
                        normalise(h)
                        if h >= 1:
                            low_prob(h - 1)
                        if h + 2 < H:
                            row_max(h + 2)
                        if h % 2 == 1 and h >= 3:
                            low_out((h - 3) // 2)
                    low_prob(H - 1)
                    low_out(HP - 1)
                    dve.wait_ge(wo_done.sem, wo_done.at(t, p, 1))
                    row = x_all[:, bass.ds(2 * t + p, 1), :].rearrange("q a d -> q (a d)")
                    dve.scalar_tensor_tensor(row, po[0:M, 0:D], gates[0:M, 0:1], row, ALU.mult, ALU.add) \
                        .then_inc(x1_done.sem, 1)

        @block.tensor
        def _(pe):
            for c in (ctr_done, qproj_done, kproj_done, vproj_done, ktr_done, score_done, ptr_done, av_done, wo_done):
                c.start(pe)

            def product(dst, terms):
                for n, (ah, al, bh, bl) in enumerate(terms):
                    pe.matmul(dst, ah, bh, start=n == 0, stop=False)
                    pe.matmul(dst, ah, bl, start=False, stop=False)
                    last = pe.matmul(dst, al, bh, start=False, stop=n == len(terms) - 1)
                return last

            pe.wait_ge(ident_set, 1)
            pe.wait_ge(small_loaded, 7 * 16)
            pe.transpose(pt[0][:, 0:4 * KD], affine_rows[:], ident[0:4 * KD, 0:4 * KD]).then_inc(affine_tr, 1)
            for b in range(B):
                pe.wait_ge(lnorm_done, B + b + 1)
                if b >= 2:
                    pe.wait_ge(lf_done, b - 1)
                for k in range(KD):
                    last = pe.transpose(sc[b % 2][:, k * M:(k + 1) * M], xn[:, b, k * P:(k + 1) * P],
                                        ident[0:M, 0:M])
                last.then_inc(ltr_done, 1)
            pe.wait_ge(lf_done, B)
            pe.wait_ge(wlo_done, 3)
            pe.wait_ge(pad_set, 3)
            with pe.Fori(0, B // 2) as t:
                for p in range(2):
                    def transpose_context(j):
                        pe.wait_ge(cnorm_done.sem, cnorm_done.at(t, p, j + 1))
                        for k in range(KD):
                            last = pe.transpose(tp[:, k * JR:(k + 1) * JR], ctx_t[:, p, j, k * P:(k + 1) * P],
                                                ident[0:JR, 0:JR])
                        last.then_inc(ctr_done.sem, 1)

                    def project(n):
                        j = ORDER[n]
                        if j == JT:
                            rows, ah, al = M, lath[:, p], latl[:, p]
                        else:
                            rows, ah, al = JR, ch[:, j], cl[:, j]
                            pe.wait_ge(cl_done.sem, cl_done.at(t, p, j + 1))
                        if n == 1:
                            pe.wait_ge(klat_done.sem, klat_done.at(t, p, 1))
                        else:
                            pe.wait_ge(rope_done.sem, rope_done.at(t, p, n - 1 if n else 0))
                        product(pk[0:rows, :], [(ah[:, k], al[:, k], wkvh[:, k, 0:INNER], wkvl[:, k, 0:INNER])
                                                for k in range(KD)]).then_inc(kproj_done.sem, 1)
                        pe.wait_ge(vl_done.sem, vl_done.at(t, p, n))
                        product(pv[0:rows, :], [(ah[:, k], al[:, k], wkvh[:, k, INNER:], wkvl[:, k, INNER:])
                                                for k in range(KD)]).then_inc(vproj_done.sem, 1)

                    def transpose_keys(n):
                        j = ORDER[n]
                        rows = M if j == JT else JR
                        if j == JT:
                            pe.wait_ge(klat_done.sem, klat_done.at(t, p, 1))
                        else:
                            pe.wait_ge(krow_done.sem, krow_done.at(t, p, j + 1))
                        for a in range(HP):
                            last = pe.transpose(tp[:, a * P:a * P + rows], krow[0:rows, j, a * P:(a + 1) * P],
                                                ident[0:rows, 0:rows])
                        last.then_inc(ktr_done.sem, 1)

                    pe.wait_ge(lat_ready.sem, lat_ready.at(t, p, 1))
                    pe.wait_ge(x1_done.sem, x1_done.at(t, p, 0))
                    for a in range(HP):
                        c = slice(a * P, (a + 1) * P)
                        last = product(po[:, a * M:(a + 1) * M],
                                       [(wqh[:, k, c], wql[:, k, c], lath[:, p, k], latl[:, p, k])
                                        for k in range(KD)])
                    last.then_inc(qproj_done.sem, 1)
                    pe.wait_ge(ktl_done.sem, ktl_done.at(t, p, 0))
                    transpose_context(0)
                    project(0)
                    pe.wait_ge(cf_done.sem, cf_done.at(t, p, 1))
                    transpose_context(1)
                    pe.wait_ge(cf_done.sem, cf_done.at(t, p, 2))
                    transpose_keys(0)
                    project(1)
                    pe.wait_ge(ktl_done.sem, ktl_done.at(t, p, 1))
                    transpose_context(2)
                    project(2)
                    pe.wait_ge(cf_done.sem, cf_done.at(t, p, 3))
                    transpose_keys(1)
                    project(3)
                    pe.wait_ge(ktl_done.sem, ktl_done.at(t, p, 2))
                    transpose_keys(2)
                    pe.wait_ge(ktl_done.sem, ktl_done.at(t, p, 3))
                    transpose_keys(3)

                    def scores(h):
                        if h == 0:
                            pe.wait_ge(ktl_done.sem, ktl_done.at(t, p, NT))
                            pe.wait_ge(ql_done.sem, ql_done.at(t, p, 1))
                        pe.wait_ge(exp_done.sem, exp_done.at(t, p, h - 1))
                        r = slice(h % 2 * DH, (h % 2 + 1) * DH)
                        a = h // 2
                        product(sc[h % 2][0:M, 0:JP], [(qh[r, p, a], ql[r, p, a], kth[r, p, a], ktl[r, p, a])]) \
                            .then_inc(score_done.sem, 1)

                    def transpose_probs(h):
                        pe.wait_ge(prob_done.sem, prob_done.at(t, p, h + 1))
                        pe.wait_ge(ptl_done.sem, ptl_done.at(t, p, h - 1))
                        for j in range(NT):
                            last = pe.transpose(pt[h % 2][0:JR, j * M:(j + 1) * M],
                                                prob[:, h % 2, j * JR:(j + 1) * JR], ident[0:M, 0:M])
                        last.then_inc(ptr_done.sem, 1)

                    def values(a):
                        pe.wait_ge(ptl_done.sem, ptl_done.at(t, p, 2 * a + 2))
                        if a == 0:
                            pe.wait_ge(vl_done.sem, vl_done.at(t, p, NT))
                        pe.wait_ge(otl_done.sem, otl_done.at(t, p, a))
                        c = slice(a * P, (a + 1) * P)
                        terms = []
                        for j in range(NT):
                            rows = M if j == JT else JR
                            terms.append((vh[0:rows, p, j, c], vl[0:rows, p, j, c],
                                          pth[0:rows, a % 2, j].rearrange("q u m -> q (u m)"),
                                          ptl[0:rows, a % 2, j].rearrange("q u m -> q (u m)")))
                        product(po[:, 0:2 * M], terms).then_inc(av_done.sem, 1)

                    scores(0)
                    scores(1)
                    for h in range(H):
                        transpose_probs(h)
                        if h + 2 < H:
                            scores(h + 2)
                        if h % 2 == 0 and h >= 2:
                            values(h // 2 - 1)
                    values(HP - 1)
                    pe.wait_ge(otl_done.sem, otl_done.at(t, p, HP))
                    product(po[0:M, 0:D], [(oth[:, a], otl[:, a], woh[:, a], wol[:, a]) for a in range(HP)]) \
                        .then_inc(wo_done.sem, 1)


def experts(nc, wg, w1, b1, w2, b2, out, probs_dram, x_all, ident, gates, neg_half, w1s, w2s,
            w1_loaded, w2_loaded):
    with ExitStack() as st:
        def sb(name, shape, dt=F32):
            return st.enter_context(nc.sbuf_tensor(name, shape, dt))

        def sem(name):
            return st.enter_context(nc.semaphore(name))

        def tally(name, per):
            return Tally(sem(name), per)

        wg_t = sb("wg_t", [P, KD, E])
        rstat, rmv = sb("rstat", [M, B, 6]), sb("rmv", [M, B, 2])
        rvar, rrstd = sb("rvar", [M, B]), sb("rrstd", [M, B])
        x2 = sb("x2", [M, B, D])
        x2f = sb("x2f", [P, KD, TOK])
        x2h, x2l = sb("x2h", [P, KD, TOK], F32R), sb("x2l", [P, KD, TOK], F32R)
        be = [M, B, E]
        logit, prob, left, hit, key, first, second, rank = (
            sb(n, be) for n in ("logit", "eprob", "left", "hit", "key", "first", "second", "rank"))
        red = sb("red", [M, 8, B])
        pnorm = sb("pnorm", be)
        pT = sb("pT", [E, TOK])
        b1rows, b1T = sb("b1rows", [E * FB, P]), sb("b1T", [P, E * FB])
        b2_t = sb("b2_t", [E, D])
        pb = sb("pb", [P, 2, 2, HALF])
        w1h, w1l = sb("w1h", [P, 2, KD, FF], F32R), sb("w1l", [P, 2, KD, FF], F32R)
        w2h, w2l = sb("w2h", [P, 2, FB, D], F32R), sb("w2l", [P, 2, FB, D], F32R)
        hf = sb("hf", [P, 2, 2, HALF])
        hh, hl = sb("hh", [P, 2, 2, HALF], F32R), sb("hl", [P, 2, 2, HALF], F32R)
        weighed = sb("weighed", [P, KD * 2, HALF])
        y = sb("y", [P, KD * 2, HALF])
        obuf = sb("obuf", [M, 2, D])
        pu = [st.enter_context(nc.psum_tensor(f"pu{n}", [P, 2, 512], F32)) for n in range(2)]
        py = [st.enter_context(nc.psum_tensor(f"py{n}", [P, 512], F32)) for n in range(4)]

        small_loaded = sem("esmall_loaded")
        rstat_done, rmv_done, rvar_done, rrstd_done, rnorm_done = (
            sem(n) for n in ("rstat_done", "rmv_done", "rvar_done", "rrstd_done", "rnorm_done"))
        rtr_done, x2f_done, x2h_done, x2l_done = (sem(n) for n in ("rtr_done", "x2f_done", "x2h_done", "x2l_done"))
        logit_done, router_step, rexp_done, pnorm_done = (
            sem(n) for n in ("logit_done", "router_step", "rexp_done", "pnorm_done"))
        ptr_done, pT_done, pT_stored, b1tr_done, b1T_done = (
            sem(n) for n in ("eptr_done", "pT_done", "pT_stored", "b1tr_done", "b1T_done"))
        b2_done, y_set = sem("b2_done"), sem("y_set")
        pb_loaded = [sem("pb_loaded0"), sem("pb_loaded1")]
        w1h_done, w1l_done, w2h_done, w2l_done = (tally(n, 1) for n in ("w1h_done", "w1l_done", "w2h_done", "w2l_done"))
        up_done, gelu_done, hh_done, hl_done, down_done = (
            tally(n, FB) for n in ("up_done", "gelu_done", "hh_done", "hl_done", "down_done"))
        weighed_done, added_done = tally("weighed_done", 4), tally("added_done", 1)
        ytr_done, out_done = sem("ytr_done"), sem("out_done")
        stored = [sem("stored0"), sem("stored1")]
        rank_set = sem("rank_set")

        block = st.enter_context(nc.Block())

        @block.sync
        def _(sp):
            sp.dma_start(wg_t[:], wg.rearrange("(k p) e -> p k e", p=P)).then_inc(small_loaded, 16)
            sp.dma_start(b1rows[:], b1.rearrange("e (f p) -> (e f) p", p=P)).then_inc(small_loaded, 16)
            sp.dma_start(b2_t[:], b2).then_inc(small_loaded, 16)
            for p in range(2):
                if p == 0:
                    sp.dma_start(w1s[:], w1[p].rearrange("(k p) f -> p k f", p=P)).then_inc(w1_loaded, 16)
                    sp.dma_start(w2s[:], w2[p].rearrange("(f p) d -> p f d", p=P)).then_inc(w2_loaded, 16)
            sp.wait_ge(pT_done, 2)
            sp.dma_start(probs_dram, pT[:]).then_inc(pT_stored, 16)
            sp.wait_ge(pT_stored, 16)

            def load_weights(t, p, e):
                sp.wait_ge(w1l_done.sem, w1l_done.at(t, p, 0))
                sp.dma_start(w1s[:], w1[e].rearrange("(k p) f -> p k f", p=P)).then_inc(w1_loaded, 16)
                sp.wait_ge(w2l_done.sem, w2l_done.at(t, p, 0))
                sp.dma_start(w2s[:], w2[e].rearrange("(f p) d -> p f d", p=P)).then_inc(w2_loaded, 16)

            def load_probs(t, p, e):
                sp.wait_ge(weighed_done.sem, weighed_done.at(t, p, -4))
                row = probs_dram[e] if isinstance(e, int) else probs_dram[bass.ds(e, 1), :].rearrange("a n -> (a n)")
                sp.dma_start(pb[:, p].rearrange("q a n -> q (a n)"),
                             row.rearrange("(a n) -> a n", a=1).broadcast_to([P, TOK])) \
                    .then_inc(pb_loaded[p], 16)

            load_probs(0, 0, 0)
            load_weights(0, 1, 1)
            load_probs(0, 1, 1)
            with sp.Fori(1, E // 2) as t:
                for p in range(2):
                    load_weights(t, p, 2 * t + p)
                    load_probs(t, p, 2 * t + p)
            for b in range(B):
                sp.wait_ge(out_done, b + 1)
                sp.dma_start(out[b], obuf[:, b % 2]).then_inc(stored[b % 2], 16)
            for n in range(2):
                sp.wait_ge(stored[n], 16 * B // 2)

        @block.gpsimd
        def _(pool):
            for c in (w1l_done, w2l_done):
                c.start(pool)
            for e in range(E):
                pool.memset(rank[:, :, e], float(E - e)).then_inc(rank_set, 1)
            pool.wait_ge(rmv_done, B)
            pool.tensor_scalar(rvar[:], rmv[:, :, 1], EPS, None, ALU.add).then_inc(rvar_done, 1)
            pool.wait_ge(rvar_done, 1)
            pool.tensor_tensor(rrstd[:], rvar[:], neg_half[0:M, :], ALU.pow).then_inc(rrstd_done, 1)
            with pool.Fori(0, E // 2) as t:
                for p in range(2):
                    pool.wait_ge(w1h_done.sem, w1h_done.at(t, p, 1))
                    pool.tensor_tensor(w1l[:, p], w1s[:], w1h[:, p].bitcast(F32), ALU.subtract) \
                        .then_inc(w1l_done.sem, 1)
                    pool.wait_ge(w2h_done.sem, w2h_done.at(t, p, 1))
                    pool.tensor_tensor(w2l[:, p], w2s[:], w2h[:, p].bitcast(F32), ALU.subtract) \
                        .then_inc(w2l_done.sem, 1)

        @block.scalar
        def _(act):
            for c in (gelu_done, hh_done):
                c.start(act)
            for b in range(B):
                act.wait_ge(x2f_done, b + 1)
                act.copy(x2h[:, :, b * M:(b + 1) * M], x2f[:, :, b * M:(b + 1) * M]).then_inc(x2h_done, 1)
            act.wait_ge(router_step, 3)
            act.activation(prob[:], left[:], ACT.Exp).then_inc(rexp_done, 1)
            act.wait_ge(b1T_done, 1)
            with act.Fori(0, E // 2) as t:
                for p in range(2):
                    for f in range(FB):
                        act.wait_ge(up_done.sem, up_done.at(t, p, f + 1))
                        act.wait_ge(hl_done.sem, hl_done.at(t, p, f - 1))
                        act.activation(hf[:, f % 2], pu[f % 2][:, :, 0:HALF], ACT.Gelu,
                                       bias=b1T[:, bass.ds(t * (2 * FB) + (p * FB + f), 1)]) \
                            .then_inc(gelu_done.sem, 1)
                        act.wait_ge(gelu_done.sem, gelu_done.at(t, p, f + 1))
                        act.wait_ge(down_done.sem, down_done.at(t, p, f - 1))
                        act.copy(hh[:, f % 2], hf[:, f % 2]).then_inc(hh_done.sem, 1)

        @block.vector
        def _(dve):
            for c in (w1h_done, w2h_done, hl_done, weighed_done, added_done):
                c.start(dve)
            for b in range(B):
                dve.bn_stats(rstat[:, b, :], x_all[:, b, :]).then_inc(rstat_done, 1)
            for b in range(B):
                dve.wait_ge(rstat_done, b + 1)
                dve.bn_aggr(rmv[:, b, :], rstat[:, b, :]).then_inc(rmv_done, 1)
            dve.wait_ge(rmv_done, B)
            dve.wait_ge(rrstd_done, 1)
            for b in range(B):
                dve.tensor_scalar(x2[:, b, :], x_all[:, b, :], rmv[:, b, 0:1], rrstd[:, b:b + 1],
                                  ALU.subtract, ALU.mult).then_inc(rnorm_done, 1)

            def low_x2(b):
                c = slice(b * M, (b + 1) * M)
                dve.wait_ge(x2h_done, b + 1)
                dve.tensor_tensor(x2l[:, :, c], x2f[:, :, c], x2h[:, :, c].bitcast(F32), ALU.subtract) \
                    .then_inc(x2l_done, 1)

            for b in range(B):
                dve.wait_ge(rtr_done, b + 1)
                c = slice(b * M, (b + 1) * M)
                dve.tensor_copy(x2f[:, :, c], py[b % 2][:, 0:KD * M].rearrange("q (k m) -> q k m", k=KD)) \
                    .then_inc(x2f_done, 1)
                if b:
                    low_x2(b - 1)
            low_x2(B - 1)
            steps = 0

            def step(ins):
                nonlocal steps
                steps += 1
                ins.then_inc(router_step, 1)
                dve.wait_ge(router_step, steps)

            def over_experts(v):
                return v.rearrange("q (b a) -> q b a", a=1).broadcast_to(be)

            dve.wait_ge(logit_done, 1)
            step(dve.tensor_copy(logit[:], py[2][0:M, 0:B * E].rearrange("q (b e) -> q b e", b=B)))
            step(dve.tensor_reduce(red[:, 0], logit[:], AX, ALU.max))
            step(dve.tensor_tensor(left[:], logit[:], over_experts(red[:, 0]), ALU.subtract))
            dve.wait_ge(rexp_done, 1)
            step(dve.tensor_reduce(red[:, 1], prob[:], AX, ALU.add))
            step(dve.reciprocal(red[:, 2], red[:, 1]))
            step(dve.tensor_tensor(prob[:], prob[:], over_experts(red[:, 2]), ALU.mult))
            dve.wait_ge(rank_set, E)

            def largest(values, onehot, r):
                step(dve.tensor_reduce(red[:, r], values, AX, ALU.max))
                step(dve.tensor_tensor(hit[:], values, over_experts(red[:, r]), ALU.is_equal))
                step(dve.tensor_tensor(key[:], hit[:], rank[:], ALU.mult))
                step(dve.tensor_reduce(red[:, r + 1], key[:], AX, ALU.max))
                step(dve.tensor_tensor(onehot, rank[:], over_experts(red[:, r + 1]), ALU.is_equal))

            largest(prob[:], first[:], 3)
            step(dve.scalar_tensor_tensor(left[:], first[:], -BIG, prob[:], ALU.mult, ALU.add))
            largest(left[:], second[:], 5)
            step(dve.tensor_tensor(hit[:], first[:], second[:], ALU.add))
            step(dve.tensor_tensor(key[:], prob[:], hit[:], ALU.mult))
            step(dve.tensor_reduce(red[:, 0], key[:], AX, ALU.add))
            step(dve.tensor_scalar(red[:, 1], red[:, 0], TOP_EPS, None, ALU.add))
            step(dve.reciprocal(red[:, 2], red[:, 1]))
            dve.tensor_tensor(pnorm[:], key[:], over_experts(red[:, 2]), ALU.mult).then_inc(pnorm_done, 1)
            for n in range(2):
                dve.wait_ge(ptr_done, n + 1)
                dve.tensor_copy(pT[:, n * HALF:(n + 1) * HALF], pu[0][0:E, n, 0:HALF]).then_inc(pT_done, 1)
            dve.wait_ge(b1tr_done, 1)
            dve.tensor_copy(b1T[:], pu[1][:, 0, 0:E * FB]).then_inc(b1T_done, 1)
            dve.wait_ge(b2_done, 1)
            for g in range(4):
                dve.tensor_copy(y[:, g], py[g][:, 0:HALF]).then_inc(y_set, 1)
            dve.wait_ge(y_set, 4)

            def split_high(t, p):
                dve.wait_ge(w1_loaded, t * 32 + 16 * (p + 1))
                dve.wait_ge(up_done.sem, up_done.at(t, p, -FB))
                dve.tensor_copy(w1h[:, p], w1s[:]).then_inc(w1h_done.sem, 1)
                dve.wait_ge(w2_loaded, t * 32 + 16 * (p + 1))
                dve.wait_ge(down_done.sem, down_done.at(t, p, -FB))
                dve.tensor_copy(w2h[:, p], w2s[:]).then_inc(w2h_done.sem, 1)

            def pair(t, final):
                for p in range(2):
                    for f in range(FB):
                        if f == 4:
                            if p == 0:
                                split_high(t, 1)
                            elif not final:
                                split_high(t + 1, 0)
                        dve.wait_ge(hh_done.sem, hh_done.at(t, p, f + 1))
                        dve.tensor_tensor(hl[:, f % 2], hf[:, f % 2], hh[:, f % 2].bitcast(F32), ALU.subtract) \
                            .then_inc(hl_done.sem, 1)
                    dve.wait_ge(pb_loaded[p], t * 16 + 16)
                    dve.wait_ge(down_done.sem, down_done.at(t, p, FB))
                    for g in range(4):
                        dve.tensor_tensor(weighed[:, g], py[g][:, 0:HALF], pb[:, p, g % 2], ALU.mult) \
                            .then_inc(weighed_done.sem, 1)
                    dve.wait_ge(weighed_done.sem, weighed_done.at(t, p, 4))
                    for g in range(4):
                        last = dve.tensor_tensor(y[:, g], y[:, g], weighed[:, g], ALU.add)
                    last.then_inc(added_done.sem, 1)
                    dve.wait_ge(added_done.sem, added_done.at(t, p, 1))

            split_high(0, 0)
            with dve.Fori(0, E // 2 - 1) as t:
                pair(t, False)
            pair(E // 2 - 1, True)
            for b in range(B):
                dve.wait_ge(ytr_done, b + 1)
                if b >= 2:
                    dve.wait_ge(stored[b % 2], 16 * (b // 2))
                dve.scalar_tensor_tensor(obuf[:, b % 2], py[b % 2][0:M, 0:D], gates[0:M, 1:2], x_all[:, b, :],
                                         ALU.mult, ALU.add).then_inc(out_done, 1)

        @block.tensor
        def _(pe):
            for c in (up_done, down_done):
                c.start(pe)
            for b in range(B):
                pe.wait_ge(rnorm_done, b + 1)
                if b >= 2:
                    pe.wait_ge(x2f_done, b - 1)
                for k in range(KD):
                    last = pe.transpose(py[b % 2][:, k * M:(k + 1) * M], x2[:, b, k * P:(k + 1) * P],
                                        ident[0:M, 0:M])
                last.then_inc(rtr_done, 1)
            pe.wait_ge(small_loaded, 48)
            for b in range(B):
                pe.wait_ge(x2f_done, b + 1)
                for k in range(KD):
                    last = pe.matmul(py[2][0:M, b * E:(b + 1) * E], x2f[:, k, b * M:(b + 1) * M], wg_t[:, k, :],
                                     start=k == 0, stop=k == KD - 1)
            last.then_inc(logit_done, 1)
            pe.transpose(pu[1][:, 0, 0:E * FB], b1rows[:], ident[0:E * FB, 0:E * FB]).then_inc(b1tr_done, 1)
            pe.wait_ge(pnorm_done, 1)
            for n in range(2):
                for b in range(B // 2):
                    last = pe.transpose(pu[0][0:E, n, b * M:(b + 1) * M], pnorm[:, n * (B // 2) + b, :],
                                        ident[0:M, 0:M])
                last.then_inc(ptr_done, 1)
            pe.wait_ge(pT_done, 2)
            for g in range(4):
                last = pe.matmul(py[g][:, 0:HALF], b2_t[:, g // 2 * P:(g // 2 + 1) * P],
                                 pT[:, g % 2 * HALF:(g % 2 + 1) * HALF], start=True, stop=True)
            last.then_inc(b2_done, 1)
            pe.wait_ge(b1T_done, 1)
            pe.wait_ge(y_set, 4)
            pe.wait_ge(x2l_done, B)

            def up(t, p, f):
                if f == 0:
                    pe.wait_ge(w1l_done.sem, w1l_done.at(t, p, 1))
                pe.wait_ge(gelu_done.sem, gelu_done.at(t, p, f - 1))
                c = slice(f * P, (f + 1) * P)
                for n in range(2):
                    s = slice(n * HALF, (n + 1) * HALF)
                    for k in range(KD):
                        pe.matmul(pu[f % 2][:, n, 0:HALF], w1h[:, p, k, c], x2h[:, k, s], start=k == 0, stop=False)
                        pe.matmul(pu[f % 2][:, n, 0:HALF], w1h[:, p, k, c], x2l[:, k, s], start=False, stop=False)
                        last = pe.matmul(pu[f % 2][:, n, 0:HALF], w1l[:, p, k, c], x2h[:, k, s], start=False,
                                         stop=k == KD - 1)
                last.then_inc(up_done.sem, 1)

            def down(t, p, f):
                if f == 0:
                    pe.wait_ge(w2l_done.sem, w2l_done.at(t, p, 1))
                    pe.wait_ge(weighed_done.sem, weighed_done.at(t, p, 0))
                pe.wait_ge(hl_done.sem, hl_done.at(t, p, f + 1))
                for g in range(4):
                    c = slice(g // 2 * P, (g // 2 + 1) * P)
                    dst = py[g][:, 0:HALF]
                    pe.matmul(dst, w2h[:, p, f, c], hh[:, f % 2, g % 2], start=f == 0, stop=False)
                    pe.matmul(dst, w2h[:, p, f, c], hl[:, f % 2, g % 2], start=False, stop=False)
                    last = pe.matmul(dst, w2l[:, p, f, c], hh[:, f % 2, g % 2], start=False, stop=f == FB - 1)
                last.then_inc(down_done.sem, 1)

            def pair(t, final):
                for p in range(2):
                    for f in range(FB):
                        if f + 1 < FB:
                            up(t, p, f + 1)
                        elif p == 0:
                            up(t, 1, 0)
                        elif not final:
                            up(t + 1, 0, 0)
                        down(t, p, f)

            up(0, 0, 0)
            with pe.Fori(0, E // 2 - 1) as t:
                pair(t, False)
            pair(E // 2 - 1, True)
            pe.wait_ge(added_done.sem, added_done.at(E // 2 - 1, 1, 1))
            for b in range(B):
                if b >= 2:
                    pe.wait_ge(out_done, b - 1)
                n, c = b // (B // 2), b % (B // 2) * M
                for k in range(KD):
                    last = pe.transpose(py[b % 2][0:M, k * P:(k + 1) * P], y[:, 2 * k + n, c:c + M], ident[:, :])
                last.then_inc(ytr_done, 1)


def rope_table(np):
    inv_freq = 1.0 / 10000.0 ** (np.arange(0, DH, 2, dtype=np.float32) / np.float32(DH))
    theta = np.arange(J, dtype=np.float32)[:, None] * inv_freq.astype(np.float32)[None, :]
    cos = np.cos(np.concatenate([theta, theta], axis=1))
    sin = np.sin(np.concatenate([-theta, theta], axis=1))
    t = np.stack([cos, sin]).reshape(2, JT, JR, DH).transpose(2, 0, 1, 3)
    return np.ascontiguousarray(t, dtype=np.float32)


_INS = ["x", "ctx_1024", "g_xattn", "g_ffn", "L0_xattn_gamma_x", "L0_xattn_beta_x", "L0_xattn_gamma_l",
        "L0_xattn_beta_l", "L0_xattn_Wq", "L0_xattn_Wkv", "L0_xattn_Wo", "L0_ffn_Wg", "L0_ffn_W1", "L0_ffn_b1",
        "L0_ffn_W2", "L0_ffn_b2"]


def kernel(**inputs):
    import numpy as np
    from concourse import bacc
    from concourse.bass_utils import run_bass_kernel_spmd

    nc = bacc.Bacc("TRN2", target_bir_lowering=False, num_devices=1)
    arrays = {f"in_{name}": np.ascontiguousarray(inputs[name]) for name in _INS}
    arrays["rope"] = rope_table(np)
    args = [nc.dram_tensor(name, a.shape, mybir.dt.from_np(a.dtype), kind="ExternalInput").ap()
            for name, a in arrays.items()]
    out = nc.dram_tensor("out", (B, M, D), F32, kind="ExternalOutput").ap()
    build_program(nc, *args, out)
    r = run_bass_kernel_spmd(nc, [arrays], core_ids=[0])
    return r.results[0]["out"]
```

```python
from contextlib import ExitStack

import concourse.bass as bass
from concourse import mybir
from concourse.alu_op_type import AluOpType as ALU

F32 = mybir.dt.float32
F32R = mybir.dt.float32r
ACT = mybir.ActivationFunctionType
AX = mybir.AxisListType.X

B, M, D = 8, 112, 256
J = 375
H, DH = 8, 64
INNER = H * DH
E, FF = 8, 1024
P = 128
KD = D // P
JT, JR = 3, J // 3
NT = JT + 1
JA = J + M
JP = JA + 1
PP = NT * JR
HP = H // 2
TOK = B * M
HALF = TOK // 2
FB = FF // P
SCALE = DH ** -0.5
EPS = 1e-5
TOP_EPS = 1e-9
BIG = 4.0


class Tally:

    def __init__(self, sem, per):
        self.sem, self.per = sem, per

    def start(self, eng):
        eng.sem_inc(self.sem, self.per + 1)

    def at(self, t, p, n):
        return t * (2 * self.per) + (self.per * (p + 1) + 1 + n)


def build_program(nc, x, ctx, g_xattn, g_ffn, gamma_x, beta_x, gamma_l, beta_l, wq, wkv, wo,
                  wg, w1, b1, w2, b2, rope, out):
    probs_dram = nc.dram_tensor("probs_scratch", [E, TOK], F32).ap()
    with ExitStack() as whole:
        def keep(name, shape, dt=F32):
            return whole.enter_context(nc.sbuf_tensor(name, shape, dt))

        x_all = keep("x_all", [M, B, D])
        ident = keep("ident", [P, P])
        gates = keep("gates", [P, 2])
        neg_half = keep("neg_half", [P, B])
        w1s = keep("w1s", [P, KD, FF])
        w2s = keep("w2s", [P, FB, D])
        tokh, tokl = keep("tokh", [P, KD, TOK], F32R), keep("tokl", [P, KD, TOK], F32R)
        x2 = keep("x2", [M, B, D])
        w1_loaded = whole.enter_context(nc.semaphore("w1_loaded"))
        w2_loaded = whole.enter_context(nc.semaphore("w2_loaded"))
        attention(nc, x, ctx, g_xattn, g_ffn, gamma_x, beta_x, gamma_l, beta_l, wq, wkv, wo, rope,
                  w1, w2, x_all, x2, tokh, tokl, ident, gates, neg_half, w1s, w2s, w1_loaded, w2_loaded)
        experts(nc, wg, w1, b1, w2, b2, out, probs_dram, x_all, x2, tokh, tokl, ident, gates, w1s, w2s,
                w1_loaded, w2_loaded)


def attention(nc, x, ctx, g_xattn, g_ffn, gamma_x, beta_x, gamma_l, beta_l, wq, wkv, wo, rope,
              w1, w2, x_all, x2, lnh, lnl, ident, gates, neg_half, w1s, w2s, w1_loaded, w2_loaded):
    with ExitStack() as st:
        def sb(name, shape, dt=F32):
            return st.enter_context(nc.sbuf_tensor(name, shape, dt))

        def ps(name):
            return st.enter_context(nc.psum_tensor(name, [P, 512], F32))

        def sem(name):
            return st.enter_context(nc.semaphore(name))

        def tally(name, per):
            return Tally(sem(name), per)

        wkvh, wkvl = sb("wkvh", [P, KD, 2 * INNER], F32R), sb("wkvl", [P, KD, 2 * INNER], F32R)
        wqh, wql = sb("wqh", [P, KD, INNER], F32R), sb("wql", [P, KD, INNER], F32R)
        woh, wol = sb("woh", [P, HP, D], F32R), sb("wol", [P, HP, D], F32R)
        affine_rows = sb("affine_rows", [4 * KD, P])
        affine = sb("affine", [P, 4, KD])
        rope_t = sb("rope_t", [JR, 2, JT, DH])
        krot = sb("krot", [JR, 4, INNER])
        kraw, kcos, ksin = krot[:, 0:2], krot[:, 2], krot[:, 3]
        xn = krot[0:M].rearrange("q a (c d) -> q (a c) d", d=D)
        lstat, lmv = sb("lstat", [M, B, 6]), sb("lmv", [M, B, 2])
        lvar, lrstd = sb("lvar", [M, B]), sb("lrstd", [M, B])
        lath, latl = sb("lath", [P, 2, KD, M], F32R), sb("latl", [P, 2, KD, M], F32R)
        qh, ql = sb("qh", [P, 2, HP, M], F32R), sb("ql", [P, 2, HP, M], F32R)
        ctx_t = sb("ctx_t", [JR, 2, JT, D])
        cstat = sb("cstat", [JR, JT, 6])
        csum, cdiff, csq, cmean = (sb(n, [JR, JT]) for n in ("csum", "cdiff", "csq", "cmean"))
        x1row = sb("x1row", [M, D])
        ostat, omean = sb("ostat", [M, 6]), sb("omean", [M, 4])
        ovar, orstd = sb("ovar", [M, 1]), sb("orstd", [M, 1])
        cvar, crstd = sb("cvar", [JR, JT]), sb("crstd", [JR, JT])
        cf = sb("cf", [P, JT, KD, JR])
        lf = cf[:, 0:2, :, 0:M]
        ch, cl = sb("ch", [P, JT, KD, JR], F32R), sb("cl", [P, JT, KD, JR], F32R)
        krow = sb("krow", [JR, NT, INNER])
        qrow = krow[0:M, JT]
        kth, ktl = sb("kth", [P, 2, HP, JP], F32R), sb("ktl", [P, 2, HP, JP], F32R)
        vh, vl = sb("vh", [JR, 2, NT, INNER], F32R), sb("vl", [JR, 2, NT, INNER], F32R)
        negmax, total, inv = sb("negmax", [M, 2]), sb("total", [M, 2]), sb("inv", [M, 2])
        prob = sb("prob", [M, 2, PP])
        pth, ptl = sb("pth", [JR, 2, NT, 2, M], F32R), sb("ptl", [JR, 2, NT, 2, M], F32R)
        oth, otl = sb("oth", [P, HP, M], F32R), sb("otl", [P, HP, M], F32R)
        tp, pk, pv, po = ps("tp"), ps("pk"), ps("pv"), ps("po")
        sc = [ps("sc0"), ps("sc1")]
        pt = [ps("pt0"), ps("pt1")]

        x_loaded, w_loaded, small_loaded = sem("x_loaded"), sem("w_loaded"), sem("small_loaded")
        wqo_loaded = sem("wqo_loaded")
        ident_set, const_set, pad_set = sem("ident_set"), sem("const_set"), sem("pad_set")
        tanh_done = sem("tanh_done")
        affine_tr, affine_done = sem("affine_tr"), sem("affine_done")
        whi_done, wlo_done = sem("whi_done"), sem("wlo_done")
        lstat_done, lmv_done, lvar_done, lrstd_done, lnorm_done = (
            sem("lstat_done"), sem("lmv_done"), sem("lvar_done"), sem("lrstd_done"), sem("lnorm_done"))
        ltr_done, lf_done, lnh_done, lnl_done = sem("ltr_done"), sem("lf_done"), sem("lnh_done"), sem("lnl_done")
        ctx_loaded = [sem("ctx_loaded0"), sem("ctx_loaded1")]
        cstat_done, cparts_done, cvar_done = tally("cstat_done", JT), tally("cparts_done", 3), tally("cvar_done", 2)
        crstd_done, cnorm_done = tally("crstd_done", 1), tally("cnorm_done", JT)
        ctr_done, cf_done = tally("ctr_done", JT), tally("cf_done", JT)
        ch_done, cl_done = tally("ch_done", JT), tally("cl_done", JT)
        lat_ready, qproj_done = tally("lat_ready", 1), tally("qproj_done", 1)
        qrow_done, qtr_done = tally("qrow_done", 1), tally("qtr_done", 1)
        qh_done, ql_done = tally("qh_done", 1), tally("ql_done", 1)
        kproj_done, vproj_done = tally("kproj_done", NT), tally("vproj_done", NT)
        kraw_done, rope_done = tally("kraw_done", JT), tally("rope_done", JT)
        krow_done, klat_done = tally("krow_done", JT), tally("klat_done", 1)
        ktr_done, kth_done, ktl_done = tally("ktr_done", NT), tally("kth_done", NT), tally("ktl_done", NT)
        vh_done, vl_done = tally("vh_done", NT), tally("vl_done", NT)
        score_done, max_done, exp_done = tally("score_done", H), tally("max_done", H), tally("exp_done", H)
        inv_done, prob_done = tally("inv_done", H), tally("prob_done", H)
        ptr_done, pth_done, ptl_done = tally("ptr_done", H), tally("pth_done", H), tally("ptl_done", H)
        av_done, oth_done, otl_done = tally("av_done", HP), tally("oth_done", HP), tally("otl_done", HP)
        wo_done, x1_done = tally("wo_done", 1), tally("x1_done", 1)
        ostat_done, oparts_done, ovar_done = tally("ostat_done", 1), tally("oparts_done", 3), tally("ovar_done", 2)
        orstd_done, x2_done = tally("orstd_done", 1), tally("x2_done", 1)

        block = st.enter_context(nc.Block())

        ORDER = [JT, 0, 1, 2]

        def key_bank(n):
            return pk if n == NT - 1 else tp

        OUTPUT_AT = (0, 5, 7)

        def frame(eng, prepare, begin, head, end, close):
            for s in range(H + 1):
                prepare(0, 0, s)
            begin(0, 0)

            def batch(t, p, previous, following):
                for h in range(H):
                    head(t, p, h, previous, following)
                end(t, p, following)

            batch(0, 0, None, (0, 1))
            with eng.Fori(0, B // 2 - 1) as t:
                batch(t, 1, (t, 0), (t + 1, 0))
                batch(t + 1, 0, (t, 1), (t + 1, 1))
            batch(B // 2 - 1, 1, (B // 2 - 1, 0), None)
            close(B // 2 - 1, 1)

        @block.sync
        def _(sp):
            sp.dma_start(x_all[:], x.rearrange("b m d -> m b d")).then_inc(x_loaded, 16)
            sp.dma_start(w1s[:, :, :], wkv.rearrange("(k p) n -> p k n", p=P)).then_inc(w_loaded, 16)
            sp.dma_start(w2s[:, 0:4, :].rearrange("p (k a) d -> p k (a d)", k=KD),
                         wq.rearrange("(k p) n -> p k n", p=P)).then_inc(wqo_loaded, 16)
            sp.dma_start(w2s[:, 4:8, :], wo.rearrange("(k p) n -> p k n", p=P)).then_inc(wqo_loaded, 16)
            with sp.Fori(0, B // 2) as t:
                for p in range(2):
                    sp.wait_ge(ctr_done.sem, ctr_done.at(t, p, -JT))
                    sp.dma_start(ctx_t[:, p], ctx[2 * t + p].rearrange("(a r) d -> r a d", a=JT)) \
                        .then_inc(ctx_loaded[p], 16)
            sp.wait_ge(wlo_done, 3)
            sp.dma_start(w1s[:], w1[0].rearrange("(k p) f -> p k f", p=P)).then_inc(w1_loaded, 16)
            sp.dma_start(w2s[:], w2[0].rearrange("(f p) d -> p f d", p=P)).then_inc(w2_loaded, 16)

        @block.gpsimd
        def _(pool):
            for c in (crstd_done, cl_done, rope_done, krow_done, orstd_done):
                c.start(pool)
            pool.dma_start(rope_t[:], rope).then_inc(small_loaded, 16)
            for n, v in enumerate((gamma_x, beta_x, gamma_l, beta_l)):
                pool.dma_start(affine_rows[n * KD:(n + 1) * KD, :], v.rearrange("(k p) -> k p", p=P)).then_inc(small_loaded, 16)
            pool.dma_start(gates[:, 0:1], g_xattn.rearrange("(a b) -> a b", b=1).broadcast_to([P, 1])) \
                .then_inc(small_loaded, 16)
            pool.dma_start(gates[:, 1:2], g_ffn.rearrange("(a b) -> a b", b=1).broadcast_to([P, 1])) \
                .then_inc(small_loaded, 16)
            pool.memset(ident[:], 0.0).then_inc(const_set, 1)
            pool.memset(neg_half[:], -0.5).then_inc(const_set, 1)
            pool.wait_ge(const_set, 2)
            pool.affine_select(out=ident[:], in_=ident[:], compare_op=ALU.not_equal, fill=1.0, base=0,
                               pattern=[[-1, P]], channel_multiplier=1).then_inc(ident_set, 1)
            for r in range(2):
                pool.wait_ge(lmv_done, B * (r + 1))
                pool.tensor_scalar(lvar[:], lmv[:, :, 1], EPS, None, ALU.add).then_inc(lvar_done, 1)
                pool.wait_ge(lvar_done, r + 1)
                pool.tensor_tensor(lrstd[:], lvar[:], neg_half[0:M, :], ALU.pow).then_inc(lrstd_done, 1)
            for b in range(B):
                pool.wait_ge(lnh_done, b + 1)
                pool.tensor_tensor(lnl[:, :, b * M:(b + 1) * M], lf[:, b % 2],
                                   lnh[:, :, b * M:(b + 1) * M].bitcast(F32), ALU.subtract).then_inc(lnl_done, 1)

            def low_context(t, p, j):
                pool.wait_ge(ch_done.sem, ch_done.at(t, p, j + 1))
                pool.tensor_tensor(cl[:, j], cf[:, j], ch[:, j].bitcast(F32), ALU.subtract) \
                    .then_inc(cl_done.sem, 1)

            def rotate(t, p, j):
                pool.wait_ge(krow_done.sem, krow_done.at(t, p, j))
                pool.wait_ge(kraw_done.sem, kraw_done.at(t, p, j + 1))
                pool.tensor_tensor(kcos.rearrange("q (h c) -> q h c", h=H),
                                   kraw[:, j % 2].rearrange("q (h c) -> q h c", h=H),
                                   rope_t[:, 0, j:j + 1, :].broadcast_to([JR, H, DH]), ALU.mult)
                pool.tensor_tensor(
                    ksin.rearrange("q (h s c) -> q h s c", h=H, s=2),
                    kraw[:, j % 2].rearrange("q (h s c) -> q h s c", h=H, s=2)[:, :, ::-1, :],
                    rope_t[:, 1, j:j + 1, :].rearrange("q a (s c) -> q a s c", s=2)
                    .broadcast_to([JR, H, 2, DH // 2]), ALU.mult).then_inc(rope_done.sem, 1)
                pool.wait_ge(rope_done.sem, rope_done.at(t, p, j + 1))
                pool.wait_ge(ktr_done.sem, ktr_done.at(t, p, j + 2 - NT))
                pool.tensor_tensor(krow[:, j], kcos, ksin, ALU.add).then_inc(krow_done.sem, 1)

            def prepare(t, p, s):
                if s == 0:
                    pool.wait_ge(cvar_done.sem, cvar_done.at(t, p, 2))
                    pool.tensor_tensor(crstd[:], cvar[:], neg_half[0:JR, 0:JT], ALU.pow).then_inc(crstd_done.sem, 1)
                if s == 2:
                    low_context(t, p, 0)
                if s == 3:
                    low_context(t, p, 1)
                if s == 4:
                    rotate(t, p, 0)
                if s == 5:
                    low_context(t, p, 2)
                    rotate(t, p, 1)
                if s == 6:
                    rotate(t, p, 2)

            def output_rstd(t, p):
                pool.wait_ge(ovar_done.sem, ovar_done.at(t, p, 2))
                pool.tensor_tensor(orstd[:], ovar[:], neg_half[0:M, 0:1], ALU.pow).then_inc(orstd_done.sem, 1)

            def head(t, p, h, previous, following):
                if following:
                    prepare(*following, h)
                if h == OUTPUT_AT[1] and previous:
                    output_rstd(*previous)

            frame(pool, prepare, lambda t, p: None, head, lambda t, p, following: None, output_rstd)

        @block.scalar
        def _(act):
            for c in (lat_ready, qrow_done, cf_done, ch_done, qh_done, kraw_done, klat_done, kth_done, vh_done, exp_done, pth_done, oth_done):
                c.start(act)
            act.wait_ge(small_loaded, 7 * 16)
            act.activation(gates[:], gates[:], ACT.Tanh).then_inc(tanh_done, 1)
            act.wait_ge(w_loaded, 16)
            act.copy(wkvh[:], w1s[:]).then_inc(whi_done, 1)
            act.wait_ge(wqo_loaded, 32)
            act.copy(wqh[:].rearrange("p k (a d) -> p (k a) d", d=D), w2s[:, 0:4, :]).then_inc(whi_done, 1)
            act.copy(woh[:], w2s[:, 4:8, :]).then_inc(whi_done, 1)
            for b in range(B):
                act.wait_ge(lf_done, b + 1)
                act.copy(lnh[:, :, b * M:(b + 1) * M], lf[:, b % 2]).then_inc(lnh_done, 1)
            act.wait_ge(lnh_done, B)
            act.wait_ge(lnl_done, B)

            def split_context(t, p, j):
                act.wait_ge(ctr_done.sem, ctr_done.at(t, p, j + 1))
                act.wait_ge(cl_done.sem, cl_done.at(t, p, j + 1 - JT))
                for k in range(KD):
                    last = act.activation(cf[:, j, k, :], tp[:, k * JR:(k + 1) * JR], ACT.Identity,
                                          scale=affine[:, 0, k:k + 1], bias=affine[:, 1, k:k + 1])
                last.then_inc(cf_done.sem, 1)
                act.wait_ge(cf_done.sem, cf_done.at(t, p, j + 1))
                act.wait_ge(vproj_done.sem, vproj_done.at(t, p, j + 2 - NT))
                act.copy(ch[:, j], cf[:, j]).then_inc(ch_done.sem, 1)

            def raw_key(t, p, j):
                act.wait_ge(kproj_done.sem, kproj_done.at(t, p, j + 2))
                act.wait_ge(krow_done.sem, krow_done.at(t, p, j - 1 if j else 0))
                act.copy(kraw[:, j % 2], pk[0:JR, :]).then_inc(kraw_done.sem, 1)

            def latent_key(t, p):
                act.wait_ge(kproj_done.sem, kproj_done.at(t, p, 1))
                act.wait_ge(qtr_done.sem, qtr_done.at(t, p, 1))
                act.copy(krow[0:M, JT], pk[0:M, :]).then_inc(klat_done.sem, 1)

            def high_value(t, p, n):
                j = ORDER[n]
                rows = M if j == JT else JR
                act.wait_ge(vproj_done.sem, vproj_done.at(t, p, n + 1))
                act.wait_ge(av_done.sem, av_done.at(t, p, -HP))
                act.copy(vh[0:rows, p, j], pv[0:rows, :]).then_inc(vh_done.sem, 1)

            def high_key(t, p, n):
                j = ORDER[n]
                rows = M if j == JT else JR
                act.wait_ge(ktr_done.sem, ktr_done.at(t, p, n + 1))
                act.wait_ge(score_done.sem, score_done.at(t, p, -H))
                act.copy(kth[:, p, :, j * JR:j * JR + rows],
                         key_bank(n)[:, 0:HP * P].rearrange("q (a r) -> q a r", a=HP)[:, :, 0:rows]) \
                    .then_inc(kth_done.sem, 1)

            def prepare(t, p, s):
                if s == 0:
                    act.wait_ge(vproj_done.sem, vproj_done.at(t, p, -NT))
                    cols = bass.ds((2 * t + p) * M, M)
                    act.copy(lath[:, p], lnh[:, :, cols].bitcast(F32))
                    act.copy(latl[:, p], lnl[:, :, cols].bitcast(F32)).then_inc(lat_ready.sem, 1)
                if s == 1:
                    act.wait_ge(qproj_done.sem, qproj_done.at(t, p, 1))
                    act.wait_ge(ktr_done.sem, ktr_done.at(t, p, 1 - NT))
                    act.mul(qrow, pk[0:M, :], SCALE).then_inc(qrow_done.sem, 1)
                if s == 2:
                    act.wait_ge(qtr_done.sem, qtr_done.at(t, p, 1))
                    act.wait_ge(score_done.sem, score_done.at(t, p, -H))
                    act.copy(qh[:, p], pv[:, 0:HP * M].rearrange("q (a r) -> q a r", a=HP)).then_inc(qh_done.sem, 1)
                    split_context(t, p, 0)
                    latent_key(t, p)
                if s == 3:
                    high_value(t, p, 0)
                    split_context(t, p, 1)
                if s == 4:
                    raw_key(t, p, 0)
                    high_value(t, p, 1)
                    high_key(t, p, 0)
                if s == 5:
                    raw_key(t, p, 1)
                    split_context(t, p, 2)
                if s == 6:
                    raw_key(t, p, 2)
                if s == 7:
                    high_value(t, p, 3)
                    high_key(t, p, 1)
                if s == 8:
                    high_key(t, p, 2)
                    high_key(t, p, 3)

            def exponent(t, p, h):
                act.wait_ge(max_done.sem, max_done.at(t, p, h + 1))
                act.wait_ge(ptr_done.sem, ptr_done.at(t, p, h - 1))
                act.activation(prob[:, h % 2, 0:JA], sc[h % 2][0:M, 0:JA], ACT.Exp,
                               bias=negmax[:, h % 2:h % 2 + 1],
                               accum_out=total[:, h % 2:h % 2 + 1]).then_inc(exp_done.sem, 1)

            def high_prob(t, p, h):
                act.wait_ge(ptr_done.sem, ptr_done.at(t, p, h + 1))
                act.wait_ge(av_done.sem, av_done.at(t, p, h // 2 - 1))
                act.copy(pth[:, h // 2 % 2, :, h % 2, :],
                         pt[h % 2][0:JR, 0:NT * M].rearrange("q (a r) -> q a r", a=NT)) \
                    .then_inc(pth_done.sem, 1)

            def high_out(t, p, a):
                act.wait_ge(av_done.sem, av_done.at(t, p, a + 1))
                act.wait_ge(wo_done.sem, wo_done.at(t, p, 0))
                for u in range(2):
                    r = slice(u * DH, (u + 1) * DH)
                    last = act.copy(oth[r, a, :], po[r, u * M:(u + 1) * M])
                last.then_inc(oth_done.sem, 1)

            def begin(t, p):
                exponent(t, p, 0)
                exponent(t, p, 1)

            def head(t, p, h, previous, following):
                if following:
                    prepare(*following, h)
                high_prob(t, p, h)
                if h in (3, 5):
                    high_out(t, p, (h - 3) // 2)
                if h + 2 < H:
                    exponent(t, p, h + 2)
                if h == 5 and following:
                    high_value(*following, 2)

            def end(t, p, following):
                high_out(t, p, HP - 2)
                if following:
                    prepare(*following, H)
                high_out(t, p, HP - 1)
                if following:
                    begin(*following)

            def prepare_first(t, p, s):
                prepare(t, p, s)
                if s == 5:
                    high_value(t, p, 2)

            frame(act, prepare_first, begin, head, end, lambda t, p: None)

        @block.vector
        def _(dve):
            for c in (cstat_done, cparts_done, cvar_done, cnorm_done, ql_done, ktl_done, vl_done,
                      max_done, inv_done, prob_done, ptl_done, otl_done, x1_done, ostat_done, oparts_done, ovar_done,
                      x2_done):
                c.start(dve)
            for w in (kth, ktl):
                dve.memset(w[:, :, :, JA:JP].bitcast(F32), 0.0).then_inc(pad_set, 1)
            dve.memset(prob[:, :, JA:PP], 0.0).then_inc(pad_set, 1)
            dve.wait_ge(x_loaded, 16)
            for r in range(2):
                src = x_all if r == 0 else xn
                if r:
                    dve.wait_ge(lnorm_done, B)
                for b in range(B):
                    dve.bn_stats(lstat[:, b, :], src[:, b, :]).then_inc(lstat_done, 1)
                for b in range(B):
                    dve.wait_ge(lstat_done, r * B + b + 1)
                    dve.bn_aggr(lmv[:, b, :], lstat[:, b, :]).then_inc(lmv_done, 1)
                dve.wait_ge(lmv_done, B * (r + 1))
                dve.wait_ge(lrstd_done, r + 1)
                for b in range(B):
                    dve.tensor_scalar(xn[:, b, :], src[:, b, :], lmv[:, b, 0:1], lrstd[:, b:b + 1],
                                      ALU.subtract, ALU.mult).then_inc(lnorm_done, 1)
            dve.wait_ge(affine_tr, 1)
            dve.tensor_copy(affine[:].rearrange("q n k -> q (n k)"), pt[0][:, 0:4 * KD]).then_inc(affine_done, 1)
            dve.wait_ge(affine_done, 1)
            for b in range(B):
                dve.wait_ge(ltr_done, b + 1)
                if b >= 2:
                    dve.wait_ge(lnl_done, b - 1)
                for k in range(KD):
                    last = dve.tensor_scalar(lf[:, b % 2, k, :], sc[b % 2][:, k * M:(k + 1) * M],
                                             affine[:, 2, k:k + 1], affine[:, 3, k:k + 1], ALU.mult, ALU.add)
                last.then_inc(lf_done, 1)
            dve.wait_ge(whi_done, 1)
            dve.tensor_tensor(wkvl[:], w1s[:], wkvh[:].bitcast(F32), ALU.subtract).then_inc(wlo_done, 1)
            dve.wait_ge(whi_done, 3)
            dve.tensor_tensor(wql[:].rearrange("p k (a d) -> p (k a) d", d=D), w2s[:, 0:4, :],
                              wqh[:].rearrange("p k (a d) -> p (k a) d", d=D).bitcast(F32),
                              ALU.subtract).then_inc(wlo_done, 1)
            dve.tensor_tensor(wol[:], w2s[:, 4:8, :], woh[:].bitcast(F32), ALU.subtract).then_inc(wlo_done, 1)
            dve.wait_ge(tanh_done, 1)

            def mean_and_variance(t, p, stat, mean, var, total_, diff, sq, stat_done, parts_done, var_done):
                dve.wait_ge(stat_done.sem, stat_done.at(t, p, stat_done.per))
                dve.tensor_tensor(total_, stat[..., 1], stat[..., 4], ALU.add).then_inc(parts_done.sem, 1)
                dve.tensor_tensor(diff, stat[..., 1], stat[..., 4], ALU.subtract).then_inc(parts_done.sem, 1)
                dve.tensor_tensor(var, stat[..., 2], stat[..., 5], ALU.add)
                dve.wait_ge(parts_done.sem, parts_done.at(t, p, 2))
                dve.tensor_tensor(sq, diff, diff, ALU.mult)
                dve.tensor_scalar(mean, total_, 0.5, None, ALU.mult).then_inc(parts_done.sem, 1)
                dve.wait_ge(parts_done.sem, parts_done.at(t, p, 3))
                dve.scalar_tensor_tensor(var, sq, D / 4.0, var, ALU.mult, ALU.add).then_inc(var_done.sem, 1)
                dve.wait_ge(var_done.sem, var_done.at(t, p, 1))
                dve.tensor_scalar(var, var, 1.0 / D, EPS, ALU.mult, ALU.add).then_inc(var_done.sem, 1)

            def low_value(t, p, n):
                j = ORDER[n]
                rows = M if j == JT else JR
                dve.wait_ge(vh_done.sem, vh_done.at(t, p, n + 1))
                dve.tensor_tensor(vl[0:rows, p, j], pv[0:rows, :], vh[0:rows, p, j].bitcast(F32),
                                  ALU.subtract).then_inc(vl_done.sem, 1)

            def low_key(t, p, n):
                j = ORDER[n]
                rows = M if j == JT else JR
                dve.wait_ge(kth_done.sem, kth_done.at(t, p, n + 1))
                c = slice(j * JR, j * JR + rows)
                dve.tensor_tensor(ktl[:, p, :, c],
                                  key_bank(n)[:, 0:HP * P].rearrange("q (a r) -> q a r", a=HP)[:, :, 0:rows],
                                  kth[:, p, :, c].bitcast(F32), ALU.subtract).then_inc(ktl_done.sem, 1)

            def prepare(t, p, s):
                if s == 0:
                    dve.wait_ge(ctx_loaded[p], t * 16 + 16)
                    for j in range(JT):
                        dve.bn_stats(cstat[:, j, :], ctx_t[:, p, j, :]).then_inc(cstat_done.sem, 1)
                    mean_and_variance(t, p, cstat[:], cmean[:], cvar[:], csum[:], cdiff[:], csq[:],
                                      cstat_done, cparts_done, cvar_done)
                if s == 1:
                    dve.wait_ge(crstd_done.sem, crstd_done.at(t, p, 1))
                    for j in range(JT):
                        dve.tensor_scalar(ctx_t[:, p, j, :], ctx_t[:, p, j, :], cmean[:, j:j + 1],
                                          crstd[:, j:j + 1], ALU.subtract, ALU.mult).then_inc(cnorm_done.sem, 1)
                if s == 2:
                    dve.wait_ge(qh_done.sem, qh_done.at(t, p, 1))
                    dve.tensor_tensor(ql[:, p], pv[:, 0:HP * M].rearrange("q (a r) -> q a r", a=HP),
                                      qh[:, p].bitcast(F32), ALU.subtract).then_inc(ql_done.sem, 1)
                if s == 3:
                    low_value(t, p, 0)
                if s == 4:
                    low_value(t, p, 1)
                    low_key(t, p, 0)
                if s == 6:
                    low_value(t, p, 2)
                if s == 7:
                    low_value(t, p, 3)
                    low_key(t, p, 1)
                if s == 8:
                    low_key(t, p, 2)
                    low_key(t, p, 3)

            def row_max(t, p, h):
                dve.wait_ge(score_done.sem, score_done.at(t, p, h + 1))
                dve.tensor_reduce(negmax[:, h % 2:h % 2 + 1], sc[h % 2][0:M, 0:JA], AX, ALU.max,
                                  negate=True).then_inc(max_done.sem, 1)

            def normalise(t, p, h):
                dve.wait_ge(exp_done.sem, exp_done.at(t, p, h + 1))
                s = slice(h % 2, h % 2 + 1)
                dve.reciprocal(inv[:, s], total[:, s]).then_inc(inv_done.sem, 1)
                dve.wait_ge(inv_done.sem, inv_done.at(t, p, h + 1))
                dve.tensor_scalar(prob[:, h % 2, 0:JA], prob[:, h % 2, 0:JA], inv[:, s], None,
                                  ALU.mult).then_inc(prob_done.sem, 1)

            def low_prob(t, p, h):
                dve.wait_ge(pth_done.sem, pth_done.at(t, p, h + 1))
                s = (slice(None), h // 2 % 2, slice(None), h % 2)
                dve.tensor_tensor(ptl[s], pt[h % 2][0:JR, 0:NT * M].rearrange("q (a r) -> q a r", a=NT),
                                  pth[s].bitcast(F32), ALU.subtract).then_inc(ptl_done.sem, 1)

            def low_out(t, p, a):
                dve.wait_ge(oth_done.sem, oth_done.at(t, p, a + 1))
                for u in range(2):
                    r = slice(u * DH, (u + 1) * DH)
                    last = dve.tensor_tensor(otl[r, a, :], po[r, u * M:(u + 1) * M],
                                             oth[r, a, :].bitcast(F32), ALU.subtract)
                last.then_inc(otl_done.sem, 1)

            def begin(t, p):
                row_max(t, p, 0)
                row_max(t, p, 1)
                normalise(t, p, 0)

            def output(t, p, part):
                row = bass.ds(2 * t + p, 1)
                if part == 0:
                    dve.wait_ge(wo_done.sem, wo_done.at(t, p, 1))
                    dve.scalar_tensor_tensor(x1row[:], po[0:M, 0:D], gates[0:M, 0:1],
                                             x_all[:, row, :].rearrange("q a d -> q (a d)"), ALU.mult, ALU.add) \
                        .then_inc(x1_done.sem, 1)
                if part == 1:
                    dve.wait_ge(x1_done.sem, x1_done.at(t, p, 1))
                    dve.bn_stats(ostat[:], x1row[:]).then_inc(ostat_done.sem, 1)
                    dve.tensor_copy(x_all[:, row, :].rearrange("q a d -> q (a d)"), x1row[:])
                    mean_and_variance(t, p, ostat[:].rearrange("q (a s) -> q a s", a=1), omean[:, 0:1], ovar[:],
                                      omean[:, 1:2], omean[:, 2:3], omean[:, 3:4],
                                      ostat_done, oparts_done, ovar_done)
                if part == 2:
                    dve.wait_ge(orstd_done.sem, orstd_done.at(t, p, 1))
                    dve.tensor_scalar(x2[:, row, :].rearrange("q a d -> q (a d)"), x1row[:],
                                      omean[:, 0:1], orstd[:], ALU.subtract, ALU.mult).then_inc(x2_done.sem, 1)

            def head(t, p, h, previous, following):
                if h + 1 < H:
                    normalise(t, p, h + 1)
                if h >= 2 and following:
                    prepare(*following, h)
                if h + 2 < H:
                    row_max(t, p, h + 2)
                if h < 2 and following:
                    prepare(*following, h)
                low_prob(t, p, h)
                if h in (3, 5):
                    low_out(t, p, (h - 3) // 2)
                if h in OUTPUT_AT and previous:
                    output(*previous, OUTPUT_AT.index(h))

            def end(t, p, following):
                low_out(t, p, HP - 2)
                if following:
                    prepare(*following, H)
                low_out(t, p, HP - 1)
                if following:
                    begin(*following)

            def close(t, p):
                for part in range(3):
                    output(t, p, part)

            frame(dve, prepare, begin, head, end, close)

        @block.tensor
        def _(pe):
            for c in (ctr_done, qproj_done, qtr_done, kproj_done, vproj_done, ktr_done, score_done, ptr_done, av_done, wo_done):
                c.start(pe)

            def product(dst, terms):
                for n, (ah, al, bh, bl) in enumerate(terms):
                    pe.matmul(dst, ah, bh, start=n == 0, stop=False)
                    pe.matmul(dst, ah, bl, start=False, stop=False)
                    last = pe.matmul(dst, al, bh, start=False, stop=n == len(terms) - 1)
                return last

            pe.wait_ge(ident_set, 1)
            pe.wait_ge(small_loaded, 7 * 16)
            pe.transpose(pt[0][:, 0:4 * KD], affine_rows[:], ident[0:4 * KD, 0:4 * KD]).then_inc(affine_tr, 1)
            for b in range(B):
                pe.wait_ge(lnorm_done, B + b + 1)
                if b >= 2:
                    pe.wait_ge(lf_done, b - 1)
                for k in range(KD):
                    last = pe.transpose(sc[b % 2][:, k * M:(k + 1) * M], xn[:, b, k * P:(k + 1) * P],
                                        ident[0:M, 0:M])
                last.then_inc(ltr_done, 1)
            pe.wait_ge(lf_done, B)
            pe.wait_ge(wlo_done, 3)
            pe.wait_ge(pad_set, 3)

            def transpose_context(t, p, j):
                pe.wait_ge(cnorm_done.sem, cnorm_done.at(t, p, j + 1))
                for k in range(KD):
                    last = pe.transpose(tp[:, k * JR:(k + 1) * JR], ctx_t[:, p, j, k * P:(k + 1) * P],
                                        ident[0:JR, 0:JR])
                last.then_inc(ctr_done.sem, 1)

            def rows_of(t, p, n):
                j = ORDER[n]
                return (M, lath[:, p], latl[:, p]) if j == JT else (JR, ch[:, j], cl[:, j])

            def project_keys(t, p, n):
                rows, ah, al = rows_of(t, p, n)
                if n:
                    pe.wait_ge(cl_done.sem, cl_done.at(t, p, n))
                if n == 0:
                    pe.wait_ge(qrow_done.sem, qrow_done.at(t, p, 1))
                elif n == 1:
                    pe.wait_ge(klat_done.sem, klat_done.at(t, p, 1))
                else:
                    pe.wait_ge(kraw_done.sem, kraw_done.at(t, p, n - 1))
                product(pk[0:rows, :], [(ah[:, k], al[:, k], wkvh[:, k, 0:INNER], wkvl[:, k, 0:INNER])
                                        for k in range(KD)]).then_inc(kproj_done.sem, 1)

            def project_values(t, p, n):
                rows, ah, al = rows_of(t, p, n)
                if n == 0:
                    pe.wait_ge(ql_done.sem, ql_done.at(t, p, 1))
                else:
                    pe.wait_ge(vl_done.sem, vl_done.at(t, p, n))
                product(pv[0:rows, :], [(ah[:, k], al[:, k], wkvh[:, k, INNER:], wkvl[:, k, INNER:])
                                        for k in range(KD)]).then_inc(vproj_done.sem, 1)

            def transpose_keys(t, p, n):
                j = ORDER[n]
                rows = M if j == JT else JR
                if j == JT:
                    pe.wait_ge(klat_done.sem, klat_done.at(t, p, 1))
                else:
                    pe.wait_ge(krow_done.sem, krow_done.at(t, p, j + 1))
                for a in range(HP):
                    last = pe.transpose(key_bank(n)[:, a * P:a * P + rows], krow[0:rows, j, a * P:(a + 1) * P],
                                        ident[0:rows, 0:rows])
                last.then_inc(ktr_done.sem, 1)

            def project_queries(t, p):
                pe.wait_ge(lat_ready.sem, lat_ready.at(t, p, 1))
                pe.wait_ge(ktl_done.sem, ktl_done.at(t, p, 0))
                product(pk[0:M, :], [(lath[:, p, k], latl[:, p, k], wqh[:, k], wql[:, k])
                                     for k in range(KD)]).then_inc(qproj_done.sem, 1)

            def transpose_queries(t, p):
                pe.wait_ge(qrow_done.sem, qrow_done.at(t, p, 1))
                pe.wait_ge(vl_done.sem, vl_done.at(t, p, 0))
                for a in range(HP):
                    last = pe.transpose(pv[:, a * M:(a + 1) * M], qrow[:, a * P:(a + 1) * P], ident[0:M, 0:M])
                last.then_inc(qtr_done.sem, 1)

            def prepare(t, p, s):
                if s == 0:
                    project_queries(t, p)
                if s == 1:
                    transpose_queries(t, p)
                    project_keys(t, p, 0)
                    transpose_context(t, p, 0)
                if s == 2:
                    pe.wait_ge(cf_done.sem, cf_done.at(t, p, 1))
                    transpose_context(t, p, 1)
                    project_values(t, p, 0)
                if s == 3:
                    project_keys(t, p, 1)
                    pe.wait_ge(cf_done.sem, cf_done.at(t, p, 2))
                    transpose_keys(t, p, 0)
                    project_values(t, p, 1)
                if s == 4:
                    project_keys(t, p, 2)
                    pe.wait_ge(ktl_done.sem, ktl_done.at(t, p, 1))
                    transpose_context(t, p, 2)
                if s == 5:
                    project_values(t, p, 2)
                    project_keys(t, p, 3)
                if s == 6:
                    pe.wait_ge(cf_done.sem, cf_done.at(t, p, 3))
                    transpose_keys(t, p, 1)
                    project_values(t, p, 3)
                if s == 7:
                    pe.wait_ge(ktl_done.sem, ktl_done.at(t, p, 2))
                    transpose_keys(t, p, 2)
                    transpose_keys(t, p, 3)

            def scores(t, p, h):
                if h == 0:
                    pe.wait_ge(ktl_done.sem, ktl_done.at(t, p, NT))
                pe.wait_ge(exp_done.sem, exp_done.at(t, p, h - 1))
                r = slice(h % 2 * DH, (h % 2 + 1) * DH)
                a = h // 2
                product(sc[h % 2][0:M, 0:JP], [(qh[r, p, a], ql[r, p, a], kth[r, p, a], ktl[r, p, a])]) \
                    .then_inc(score_done.sem, 1)

            def transpose_probs(t, p, h):
                pe.wait_ge(prob_done.sem, prob_done.at(t, p, h + 1))
                pe.wait_ge(ptl_done.sem, ptl_done.at(t, p, h - 1))
                for j in range(NT):
                    last = pe.transpose(pt[h % 2][0:JR, j * M:(j + 1) * M],
                                        prob[:, h % 2, j * JR:(j + 1) * JR], ident[0:M, 0:M])
                last.then_inc(ptr_done.sem, 1)

            def values(t, p, a):
                pe.wait_ge(ptl_done.sem, ptl_done.at(t, p, 2 * a + 2))
                if a == 0:
                    pe.wait_ge(x1_done.sem, x1_done.at(t, p, 0))
                else:
                    pe.wait_ge(otl_done.sem, otl_done.at(t, p, a))
                c = slice(a * P, (a + 1) * P)
                terms = []
                for j in range(NT):
                    rows = M if j == JT else JR
                    terms.append((vh[0:rows, p, j, c], vl[0:rows, p, j, c],
                                  pth[0:rows, a % 2, j].rearrange("q u m -> q (u m)"),
                                  ptl[0:rows, a % 2, j].rearrange("q u m -> q (u m)")))
                product(po[:, 0:2 * M], terms).then_inc(av_done.sem, 1)

            def begin(t, p):
                scores(t, p, 0)
                scores(t, p, 1)

            def head(t, p, h, previous, following):
                transpose_probs(t, p, h)
                if h + 2 < H:
                    scores(t, p, h + 2)
                if h in (2, 4, 7):
                    values(t, p, {2: 0, 4: 1, 7: 2}[h])
                if following:
                    prepare(*following, h)

            def end(t, p, following):
                values(t, p, HP - 1)
                if following:
                    begin(*following)
                pe.wait_ge(otl_done.sem, otl_done.at(t, p, HP))
                product(po[0:M, 0:D], [(oth[:, a], otl[:, a], woh[:, a], wol[:, a]) for a in range(HP)]) \
                    .then_inc(wo_done.sem, 1)

            frame(pe, prepare, begin, head, end, lambda t, p: None)


def experts(nc, wg, w1, b1, w2, b2, out, probs_dram, x_all, x2, x2h, x2l, ident, gates, w1s, w2s,
            w1_loaded, w2_loaded):
    with ExitStack() as st:
        def sb(name, shape, dt=F32):
            return st.enter_context(nc.sbuf_tensor(name, shape, dt))

        def sem(name):
            return st.enter_context(nc.semaphore(name))

        def tally(name, per):
            return Tally(sem(name), per)

        wg_t = sb("wg_t", [P, KD, E])
        wgh, wgl = sb("wgh", [P, KD, E], F32R), sb("wgl", [P, KD, E], F32R)
        be = [M, B, E]
        logit, prob, left, hit, key, first, second, rank = (
            sb(n, be) for n in ("logit", "eprob", "left", "hit", "key", "first", "second", "rank"))
        red = sb("red", [M, 8, B])
        pnorm = sb("pnorm", be)
        pT = sb("pT", [E, TOK])
        b1rows, b1T = sb("b1rows", [E * FB, P]), sb("b1T", [P, E * FB])
        b2_t = sb("b2_t", [E, D])
        pb = sb("pb", [P, 2, 2, HALF])
        w1h, w1l = sb("w1h", [P, 2, KD, FF], F32R), sb("w1l", [P, 2, KD, FF], F32R)
        w2h, w2l = sb("w2h", [P, 2, FB, D], F32R), sb("w2l", [P, 2, FB, D], F32R)
        hf = sb("hf", [P, 2, 2, HALF])
        hh, hl = sb("hh", [P, 2, 2, HALF], F32R), sb("hl", [P, 2, 2, HALF], F32R)
        weighed = sb("weighed", [P, KD * 2, HALF])
        y = sb("y", [P, KD * 2, HALF])
        obuf = sb("obuf", [M, 2, D])
        pu = [st.enter_context(nc.psum_tensor(f"pu{n}", [P, 2, 512], F32)) for n in range(2)]
        py = [st.enter_context(nc.psum_tensor(f"py{n}", [P, 512], F32)) for n in range(4)]

        small_loaded = sem("esmall_loaded")
        wg_done = sem("wg_done")
        rtr_done, x2h_done, x2l_done = (sem(n) for n in ("rtr_done", "x2h_done", "x2l_done"))
        logit_done, router_step, rexp_done, pnorm_done = (
            sem(n) for n in ("logit_done", "router_step", "rexp_done", "pnorm_done"))
        ptr_done, pT_done, pT_stored, b1tr_done, b1T_done = (
            sem(n) for n in ("eptr_done", "pT_done", "pT_stored", "b1tr_done", "b1T_done"))
        b2_done, y_set = sem("b2_done"), sem("y_set")
        pb_loaded = [sem("pb_loaded0"), sem("pb_loaded1")]
        w1h_done, w1l_done, w2h_done, w2l_done = (tally(n, 1) for n in ("w1h_done", "w1l_done", "w2h_done", "w2l_done"))
        up_done, gelu_done, hh_done, hl_done, down_done = (
            tally(n, FB) for n in ("up_done", "gelu_done", "hh_done", "hl_done", "down_done"))
        weighed_done, added_done = tally("weighed_done", 4), tally("added_done", 1)
        ytr_done, out_done = sem("ytr_done"), sem("out_done")
        stored = [sem("stored0"), sem("stored1")]
        rank_set = sem("rank_set")

        block = st.enter_context(nc.Block())

        @block.sync
        def _(sp):
            sp.dma_start(wg_t[:], wg.rearrange("(k p) e -> p k e", p=P)).then_inc(small_loaded, 16)
            sp.dma_start(b1rows[:], b1.rearrange("e (f p) -> (e f) p", p=P)).then_inc(small_loaded, 16)
            sp.dma_start(b2_t[:], b2).then_inc(small_loaded, 16)
            sp.wait_ge(pT_done, 2)
            sp.dma_start(probs_dram, pT[:]).then_inc(pT_stored, 16)
            sp.wait_ge(pT_stored, 16)

            def load_weights(t, p, e):
                sp.wait_ge(w1l_done.sem, w1l_done.at(t, p, 0))
                sp.dma_start(w1s[:], w1[e].rearrange("(k p) f -> p k f", p=P)).then_inc(w1_loaded, 16)
                sp.wait_ge(w2l_done.sem, w2l_done.at(t, p, 0))
                sp.dma_start(w2s[:], w2[e].rearrange("(f p) d -> p f d", p=P)).then_inc(w2_loaded, 16)

            def load_probs(t, p, e):
                sp.wait_ge(weighed_done.sem, weighed_done.at(t, p, -4))
                row = probs_dram[e] if isinstance(e, int) else probs_dram[bass.ds(e, 1), :].rearrange("a n -> (a n)")
                sp.dma_start(pb[:, p].rearrange("q a n -> q (a n)"),
                             row.rearrange("(a n) -> a n", a=1).broadcast_to([P, TOK])) \
                    .then_inc(pb_loaded[p], 16)

            load_probs(0, 0, 0)
            load_weights(0, 1, 1)
            load_probs(0, 1, 1)
            with sp.Fori(1, E // 2) as t:
                for p in range(2):
                    load_weights(t, p, 2 * t + p)
                    load_probs(t, p, 2 * t + p)
            for b in range(B):
                sp.wait_ge(out_done, b + 1)
                sp.dma_start(out[b], obuf[:, b % 2]).then_inc(stored[b % 2], 16)
            for n in range(2):
                sp.wait_ge(stored[n], 16 * B // 2)

        @block.gpsimd
        def _(pool):
            for c in (w1l_done, w2l_done, added_done):
                c.start(pool)
            for e in range(E):
                pool.memset(rank[:, :, e], float(E - e)).then_inc(rank_set, 1)
            def low_weights(t, p):
                pool.wait_ge(w1h_done.sem, w1h_done.at(t, p, 1))
                pool.tensor_tensor(w1l[:, p], w1s[:], w1h[:, p].bitcast(F32), ALU.subtract) \
                    .then_inc(w1l_done.sem, 1)
                pool.wait_ge(w2h_done.sem, w2h_done.at(t, p, 1))
                pool.tensor_tensor(w2l[:, p], w2s[:], w2h[:, p].bitcast(F32), ALU.subtract) \
                    .then_inc(w2l_done.sem, 1)

            def add(t, p):
                pool.wait_ge(weighed_done.sem, weighed_done.at(t, p, 4))
                pool.wait_ge(added_done.sem, added_done.at(t, p, 0))
                pool.tensor_tensor(y[:], y[:], weighed[:], ALU.add).then_inc(added_done.sem, 1)

            low_weights(0, 0)
            pool.wait_ge(y_set, 4)
            with pool.Fori(0, E // 2 - 1) as t:
                low_weights(t, 1)
                add(t, 0)
                low_weights(t + 1, 0)
                add(t, 1)
            low_weights(E // 2 - 1, 1)
            add(E // 2 - 1, 0)
            add(E // 2 - 1, 1)

        @block.scalar
        def _(act):
            for c in (gelu_done, hh_done):
                c.start(act)
            for b in range(B):
                act.wait_ge(rtr_done, b + 1)
                act.copy(x2h[:, :, b * M:(b + 1) * M],
                         py[b % 3][:, 0:KD * M].rearrange("q (k m) -> q k m", k=KD)).then_inc(x2h_done, 1)
            act.wait_ge(router_step, 3)
            act.activation(prob[:], left[:], ACT.Exp).then_inc(rexp_done, 1)
            act.wait_ge(b1T_done, 1)
            with act.Fori(0, E // 2) as t:
                for p in range(2):
                    for f in range(FB):
                        act.wait_ge(up_done.sem, up_done.at(t, p, f + 1))
                        act.wait_ge(hl_done.sem, hl_done.at(t, p, f - 1))
                        act.activation(hf[:, f % 2], pu[f % 2][:, :, 0:HALF], ACT.Gelu,
                                       bias=b1T[:, bass.ds(t * (2 * FB) + (p * FB + f), 1)]) \
                            .then_inc(gelu_done.sem, 1)
                        act.wait_ge(gelu_done.sem, gelu_done.at(t, p, f + 1))
                        act.wait_ge(down_done.sem, down_done.at(t, p, f - 1))
                        act.copy(hh[:, f % 2], hf[:, f % 2]).then_inc(hh_done.sem, 1)

        @block.vector
        def _(dve):
            for c in (w1h_done, w2h_done, hl_done, weighed_done):
                c.start(dve)

            def split_high(t, p):
                dve.wait_ge(w1_loaded, t * 32 + 16 * (p + 1))
                dve.wait_ge(up_done.sem, up_done.at(t, p, -FB))
                dve.tensor_copy(w1h[:, p], w1s[:]).then_inc(w1h_done.sem, 1)
                dve.wait_ge(w2_loaded, t * 32 + 16 * (p + 1))
                dve.wait_ge(down_done.sem, down_done.at(t, p, -FB))
                dve.tensor_copy(w2h[:, p], w2s[:]).then_inc(w2h_done.sem, 1)

            dve.wait_ge(small_loaded, 48)
            dve.tensor_copy(wgh[:], wg_t[:]).then_inc(wg_done, 1)
            dve.wait_ge(wg_done, 1)
            dve.tensor_tensor(wgl[:], wg_t[:], wgh[:].bitcast(F32), ALU.subtract).then_inc(wg_done, 1)
            for b in range(B):
                c = slice(b * M, (b + 1) * M)
                dve.wait_ge(x2h_done, b + 1)
                dve.tensor_tensor(x2l[:, :, c], py[b % 3][:, 0:KD * M].rearrange("q (k m) -> q k m", k=KD),
                                  x2h[:, :, c].bitcast(F32), ALU.subtract).then_inc(x2l_done, 1)
            split_high(0, 0)
            steps = 0

            def step(ins):
                nonlocal steps
                steps += 1
                ins.then_inc(router_step, 1)
                dve.wait_ge(router_step, steps)

            def over_experts(v):
                return v.rearrange("q (b a) -> q b a", a=1).broadcast_to(be)

            dve.wait_ge(b1tr_done, 1)
            dve.tensor_copy(b1T[:], py[2][:, 0:E * FB]).then_inc(b1T_done, 1)
            dve.wait_ge(logit_done, 1)
            step(dve.tensor_copy(logit[:], py[3][0:M, 0:B * E].rearrange("q (b e) -> q b e", b=B)))
            step(dve.tensor_reduce(red[:, 0], logit[:], AX, ALU.max))
            step(dve.tensor_tensor(left[:], logit[:], over_experts(red[:, 0]), ALU.subtract))
            dve.wait_ge(rexp_done, 1)
            step(dve.tensor_reduce(red[:, 1], prob[:], AX, ALU.add))
            step(dve.reciprocal(red[:, 2], red[:, 1]))
            step(dve.tensor_tensor(prob[:], prob[:], over_experts(red[:, 2]), ALU.mult))
            dve.wait_ge(rank_set, E)

            def largest(values, onehot, r):
                step(dve.tensor_reduce(red[:, r], values, AX, ALU.max))
                step(dve.tensor_tensor(hit[:], values, over_experts(red[:, r]), ALU.is_equal))
                step(dve.tensor_tensor(key[:], hit[:], rank[:], ALU.mult))
                step(dve.tensor_reduce(red[:, r + 1], key[:], AX, ALU.max))
                step(dve.tensor_tensor(onehot, rank[:], over_experts(red[:, r + 1]), ALU.is_equal))

            largest(prob[:], first[:], 3)
            step(dve.scalar_tensor_tensor(left[:], first[:], -BIG, prob[:], ALU.mult, ALU.add))
            largest(left[:], second[:], 5)
            step(dve.tensor_tensor(hit[:], first[:], second[:], ALU.add))
            step(dve.tensor_tensor(key[:], prob[:], hit[:], ALU.mult))
            step(dve.tensor_reduce(red[:, 0], key[:], AX, ALU.add))
            step(dve.tensor_scalar(red[:, 1], red[:, 0], TOP_EPS, None, ALU.add))
            step(dve.reciprocal(red[:, 2], red[:, 1]))
            dve.tensor_tensor(pnorm[:], key[:], over_experts(red[:, 2]), ALU.mult).then_inc(pnorm_done, 1)
            for n in range(2):
                dve.wait_ge(ptr_done, n + 1)
                dve.tensor_copy(pT[:, n * HALF:(n + 1) * HALF], py[n][0:E, 0:HALF]).then_inc(pT_done, 1)
            dve.wait_ge(b2_done, 1)
            for g in range(4):
                dve.tensor_copy(y[:, g], py[g][:, 0:HALF]).then_inc(y_set, 1)
            dve.wait_ge(y_set, 4)

            def low_hidden(t, p, f):
                dve.wait_ge(hh_done.sem, hh_done.at(t, p, f + 1))
                dve.tensor_tensor(hl[:, f % 2], hf[:, f % 2], hh[:, f % 2].bitcast(F32), ALU.subtract) \
                    .then_inc(hl_done.sem, 1)

            def pair(t, final):
                for p in range(2):
                    for f in range(1, FB + 1):
                        if f < FB:
                            low_hidden(t, p, f)
                        elif p == 0:
                            low_hidden(t, 1, 0)
                        elif not final:
                            low_hidden(t + 1, 0, 0)
                        if f == 4:
                            if p == 0:
                                split_high(t, 1)
                            elif not final:
                                split_high(t + 1, 0)
                    dve.wait_ge(pb_loaded[p], t * 16 + 16)
                    dve.wait_ge(down_done.sem, down_done.at(t, p, FB))
                    dve.wait_ge(added_done.sem, added_done.at(t, p, 0))
                    for g in range(4):
                        dve.tensor_tensor(weighed[:, g], py[g][:, 0:HALF], pb[:, p, g % 2], ALU.mult) \
                            .then_inc(weighed_done.sem, 1)

            low_hidden(0, 0, 0)
            with dve.Fori(0, E // 2 - 1) as t:
                pair(t, False)
            pair(E // 2 - 1, True)
            for b in range(B):
                dve.wait_ge(ytr_done, b + 1)
                if b >= 2:
                    dve.wait_ge(stored[b % 2], 16 * (b // 2))
                dve.scalar_tensor_tensor(obuf[:, b % 2], py[b % 2][0:M, 0:D], gates[0:M, 1:2], x_all[:, b, :],
                                         ALU.mult, ALU.add).then_inc(out_done, 1)

        @block.tensor
        def _(pe):
            for c in (up_done, down_done):
                c.start(pe)
            for b in range(B):
                if b >= 3:
                    pe.wait_ge(x2l_done, b - 2)
                for k in range(KD):
                    last = pe.transpose(py[b % 3][:, k * M:(k + 1) * M], x2[:, b, k * P:(k + 1) * P],
                                        ident[0:M, 0:M])
                last.then_inc(rtr_done, 1)
            pe.wait_ge(wg_done, 2)
            for b in range(B):
                c = slice(b * M, (b + 1) * M)
                pe.wait_ge(x2l_done, b + 1)
                dst = py[3][0:M, b * E:(b + 1) * E]
                for k in range(KD):
                    pe.matmul(dst, x2h[:, k, c], wgh[:, k, :], start=k == 0, stop=False)
                    pe.matmul(dst, x2h[:, k, c], wgl[:, k, :], start=False, stop=False)
                    last = pe.matmul(dst, x2l[:, k, c], wgh[:, k, :], start=False, stop=k == KD - 1)
            last.then_inc(logit_done, 1)
            pe.wait_ge(small_loaded, 48)
            pe.transpose(py[2][:, 0:E * FB], b1rows[:], ident[0:E * FB, 0:E * FB]).then_inc(b1tr_done, 1)

            def up(t, p, f):
                if f == 0:
                    pe.wait_ge(w1l_done.sem, w1l_done.at(t, p, 1))
                pe.wait_ge(gelu_done.sem, gelu_done.at(t, p, f - 1))
                c = slice(f * P, (f + 1) * P)
                for n in range(2):
                    s = slice(n * HALF, (n + 1) * HALF)
                    for k in range(KD):
                        pe.matmul(pu[f % 2][:, n, 0:HALF], w1h[:, p, k, c], x2h[:, k, s], start=k == 0, stop=False)
                        pe.matmul(pu[f % 2][:, n, 0:HALF], w1h[:, p, k, c], x2l[:, k, s], start=False, stop=False)
                        last = pe.matmul(pu[f % 2][:, n, 0:HALF], w1l[:, p, k, c], x2h[:, k, s], start=False,
                                         stop=k == KD - 1)
                last.then_inc(up_done.sem, 1)

            def down(t, p, f):
                if f == 0:
                    pe.wait_ge(w2l_done.sem, w2l_done.at(t, p, 1))
                pe.wait_ge(hl_done.sem, hl_done.at(t, p, f + 1))
                for g in range(4):
                    c = slice(g // 2 * P, (g // 2 + 1) * P)
                    dst = py[g][:, 0:HALF]
                    if f == 0:
                        pe.wait_ge(weighed_done.sem, weighed_done.at(t, p, g + 1 - 4))
                    pe.matmul(dst, w2h[:, p, f, c], hh[:, f % 2, g % 2], start=f == 0, stop=False)
                    pe.matmul(dst, w2h[:, p, f, c], hl[:, f % 2, g % 2], start=False, stop=False)
                    last = pe.matmul(dst, w2l[:, p, f, c], hh[:, f % 2, g % 2], start=False, stop=f == FB - 1)
                last.then_inc(down_done.sem, 1)

            def pair(t, final):
                for p in range(2):
                    for f in range(FB):
                        if f + 2 < FB:
                            up(t, p, f + 2)
                        elif p == 0:
                            up(t, 1, f + 2 - FB)
                        elif not final:
                            up(t + 1, 0, f + 2 - FB)
                        down(t, p, f)

            up(0, 0, 0)
            up(0, 0, 1)
            pe.wait_ge(pnorm_done, 1)
            for n in range(2):
                for b in range(B // 2):
                    last = pe.transpose(py[n][0:E, b * M:(b + 1) * M], pnorm[:, n * (B // 2) + b, :],
                                        ident[0:M, 0:M])
                last.then_inc(ptr_done, 1)
            pe.wait_ge(pT_done, 2)
            for g in range(4):
                last = pe.matmul(py[g][:, 0:HALF], b2_t[:, g // 2 * P:(g // 2 + 1) * P],
                                 pT[:, g % 2 * HALF:(g % 2 + 1) * HALF], start=True, stop=True)
            last.then_inc(b2_done, 1)
            pe.wait_ge(y_set, 4)
            with pe.Fori(0, E // 2 - 1) as t:
                pair(t, False)
            pair(E // 2 - 1, True)
            pe.wait_ge(added_done.sem, added_done.at(E // 2 - 1, 1, 1))
            for b in range(B):
                if b >= 2:
                    pe.wait_ge(out_done, b - 1)
                n, c = b // (B // 2), b % (B // 2) * M
                for k in range(KD):
                    last = pe.transpose(py[b % 2][0:M, k * P:(k + 1) * P], y[:, 2 * k + n, c:c + M], ident[:, :])
                last.then_inc(ytr_done, 1)


def rope_table(np):
    inv_freq = 1.0 / 10000.0 ** (np.arange(0, DH, 2, dtype=np.float32) / np.float32(DH))
    theta = np.arange(J, dtype=np.float32)[:, None] * inv_freq.astype(np.float32)[None, :]
    cos = np.cos(np.concatenate([theta, theta], axis=1))
    sin = np.sin(np.concatenate([-theta, theta], axis=1))
    t = np.stack([cos, sin]).reshape(2, JT, JR, DH).transpose(2, 0, 1, 3)
    return np.ascontiguousarray(t, dtype=np.float32)


_INS = ["x", "ctx_1024", "g_xattn", "g_ffn", "L0_xattn_gamma_x", "L0_xattn_beta_x", "L0_xattn_gamma_l",
        "L0_xattn_beta_l", "L0_xattn_Wq", "L0_xattn_Wkv", "L0_xattn_Wo", "L0_ffn_Wg", "L0_ffn_W1", "L0_ffn_b1",
        "L0_ffn_W2", "L0_ffn_b2"]


def kernel(**inputs):
    import numpy as np
    from concourse import bacc
    from concourse.bass_utils import run_bass_kernel_spmd

    nc = bacc.Bacc("TRN2", target_bir_lowering=False, num_devices=1)
    arrays = {f"in_{name}": np.ascontiguousarray(inputs[name]) for name in _INS}
    arrays["rope"] = rope_table(np)
    args = [nc.dram_tensor(name, a.shape, mybir.dt.from_np(a.dtype), kind="ExternalInput").ap()
            for name, a in arrays.items()]
    out = nc.dram_tensor("out", (B, M, D), F32, kind="ExternalOutput").ap()
    build_program(nc, *args, out)
    r = run_bass_kernel_spmd(nc, [arrays], core_ids=[0])
    return r.results[0]["out"]
```

```python
from contextlib import ExitStack

import concourse.bass as bass
from concourse import mybir
from concourse.alu_op_type import AluOpType as ALU

F32 = mybir.dt.float32
F32R = mybir.dt.float32r
ACT = mybir.ActivationFunctionType
AX = mybir.AxisListType.X

B, M, D = 8, 112, 256
J = 375
H, DH = 8, 64
INNER = H * DH
E, FF = 8, 1024
P = 128
KD = D // P
JT, JR = 3, J // 3
NT = JT + 1
JA = J + M
JP = JA + 1
PP = NT * JR
HP = H // 2
TOK = B * M
HALF = TOK // 2
FB = FF // P
SCALE = DH ** -0.5
EPS = 1e-5
TOP_EPS = 1e-9
BIG = 4.0


class Tally:

    def __init__(self, sem, per):
        self.sem, self.per = sem, per

    def start(self, eng):
        eng.sem_inc(self.sem, self.per + 1)

    def at(self, t, p, n):
        return t * (2 * self.per) + (self.per * (p + 1) + 1 + n)


def build_program(nc, x, ctx, g_xattn, g_ffn, gamma_x, beta_x, gamma_l, beta_l, wq, wkv, wo,
                  wg, w1, b1, w2, b2, rope, out):
    probs_dram = nc.dram_tensor("probs_scratch", [E, TOK], F32).ap()
    with ExitStack() as whole:
        def keep(name, shape, dt=F32):
            return whole.enter_context(nc.sbuf_tensor(name, shape, dt))

        x_all = keep("x_all", [M, B, D])
        ident = keep("ident", [P, P])
        gates = keep("gates", [P, 2])
        neg_half = keep("neg_half", [P, B])
        w1s = keep("w1s", [P, KD, FF])
        w2s = keep("w2s", [P, FB, D])
        tokh, tokl = keep("tokh", [P, KD, TOK], F32R), keep("tokl", [P, KD, TOK], F32R)
        x2 = keep("x2", [M, B, D])
        wide = keep("wide_h", [P, KD, FF], F32R), keep("wide_l", [P, KD, FF], F32R)
        deep = keep("deep_h", [P, FB, D], F32R), keep("deep_l", [P, FB, D], F32R)
        logit = keep("logit", [M, B, E])

        def sem(name):
            return whole.enter_context(nc.semaphore(name))

        weights = {n: sem(n) for n in ("w1_loaded", "w2_loaded")}
        weights |= {n: Tally(sem(n), 1) for n in ("w1h_done", "w1l_done")}
        weights |= {n: Tally(sem(n), 2) for n in ("w2h_done", "w2l_done")}
        attention(nc, x, ctx, g_xattn, g_ffn, gamma_x, beta_x, gamma_l, beta_l, wq, wkv, wo, rope,
                  wg, w1, w2, x_all, x2, tokh, tokl, ident, gates, neg_half, w1s, w2s, wide, deep, logit,
                  **weights)
        experts(nc, w1, b1, w2, b2, out, probs_dram, x_all, tokh, tokl, ident, gates, w1s, w2s, wide, deep,
                logit, **weights)


def attention(nc, x, ctx, g_xattn, g_ffn, gamma_x, beta_x, gamma_l, beta_l, wq, wkv, wo, rope,
              wg, w1, w2, x_all, x2, tokh, tokl, ident, gates, neg_half, w1s, w2s, wide, deep, logit,
              w1_loaded, w2_loaded, w1h_done, w1l_done, w2h_done, w2l_done):
    with ExitStack() as st:
        def sb(name, shape, dt=F32):
            return st.enter_context(nc.sbuf_tensor(name, shape, dt))

        def ps(name):
            return st.enter_context(nc.psum_tensor(name, [P, 512], F32))

        def sem(name):
            return st.enter_context(nc.semaphore(name))

        def tally(name, per):
            return Tally(sem(name), per)

        wkvh, wkvl = wide
        wqh, wql = (w[:, 0:4, :].rearrange("p (k a) d -> p k (a d)", k=KD) for w in deep)
        woh, wol = (w[:, 4:8, :] for w in deep)
        wg_t, wgh, wgl = sb("wg_t", [P, KD, E]), sb("wgh", [P, KD, E], F32R), sb("wgl", [P, KD, E], F32R)
        affine_rows = sb("affine_rows", [4 * KD, P])
        affine = sb("affine", [P, 4, KD])
        rope_t = sb("rope_t", [JR, 2, JT, DH])
        krot = sb("krot", [JR, 2, INNER])
        kcos, ksin = krot[:, 0], krot[:, 1]
        xn = x2
        lstat, lmv = sb("lstat", [M, B, 6]), sb("lmv", [M, B, 2])
        lvar, lrstd = sb("lvar", [M, B]), sb("lrstd", [M, B])
        lath, latl = sb("lath", [P, 2, KD, M], F32R), sb("latl", [P, 2, KD, M], F32R)
        qh, ql = sb("qh", [P, 2, HP, M], F32R), sb("ql", [P, 2, HP, M], F32R)
        ctx_t = sb("ctx_t", [JR, 2, JT, D])
        cstat = sb("cstat", [JR, JT, 6])
        csum, cdiff, csq, cmean = (sb(n, [JR, JT]) for n in ("csum", "cdiff", "csq", "cmean"))
        x1row = sb("x1row", [M, D])
        ostat, omean = sb("ostat", [M, 6]), sb("omean", [M, 4])
        ovar, orstd = sb("ovar", [M, 1]), sb("orstd", [M, 1])
        cvar, crstd = sb("cvar", [JR, JT]), sb("crstd", [JR, JT])
        cf = sb("cf", [P, JT, KD, JR])
        ch, cl = sb("ch", [P, JT, KD, JR], F32R), sb("cl", [P, JT, KD, JR], F32R)
        krow = sb("krow", [JR, NT, INNER])
        qrow = krow[0:M, JT]
        kth, ktl = sb("kth", [P, 2, HP, JP], F32R), sb("ktl", [P, 2, HP, JP], F32R)
        vh, vl = sb("vh", [JR, 2, NT, INNER], F32R), sb("vl", [JR, 2, NT, INNER], F32R)
        negmax, total, inv = sb("negmax", [M, 2]), sb("total", [M, 2]), sb("inv", [M, 2])
        prob = sb("prob", [M, 2, PP])
        pth, ptl = sb("pth", [JR, 2, NT, 2, M], F32R), sb("ptl", [JR, 2, NT, 2, M], F32R)
        oth, otl = sb("oth", [P, HP, M], F32R), sb("otl", [P, HP, M], F32R)
        lf = [sb(f"lf{n}", [P, KD, M])[:] for n in range(2)]
        tp, pk, pv, po = ps("tp"), ps("pk"), ps("pv"), ps("po")
        sc = [ps("sc0"), ps("sc1")]
        pt = [ps("pt0"), ps("pt1")]

        x0_loaded, x_loaded, small_loaded = sem("x0_loaded"), sem("x_loaded"), sem("small_loaded")
        affine_loaded = sem("affine_loaded")
        wq_loaded, wkv_loaded, wo_loaded = sem("wq_loaded"), sem("wkv_loaded"), sem("wo_loaded")
        ident_set, const_set, pad_set = sem("ident_set"), sem("const_set"), sem("pad_set")
        tanh_done = sem("tanh_done")
        affine_tr, affine_done = sem("affine_tr"), sem("affine_done")
        wg_done, turned, turnh_done, turnl_done, logit_done = (
            sem(n) for n in ("wg_done", "turned", "turnh_done", "turnl_done", "logit_done"))
        whi_done, woh_done = sem("whi_done"), sem("woh_done")
        wql_done, wkl_done, wvl_done, wol_done = (sem(n) for n in ("wql_done", "wkl_done", "wvl_done", "wol_done"))
        lstat_done, lmv_done, lvar_done, lrstd_done, lnorm_done = (
            sem("lstat_done"), sem("lmv_done"), sem("lvar_done"), sem("lrstd_done"), sem("lnorm_done"))
        ltr_done, lnh_done, lnl_done = sem("ltr_done"), sem("lnh_done"), sem("lnl_done")
        lf_done = [sem("lf_even_done"), sem("lf_odd_done")]
        ctx_loaded = [sem("ctx_loaded0"), sem("ctx_loaded1")]
        cstat_done, cparts_done, cvar_done = tally("cstat_done", JT), tally("cparts_done", 3), tally("cvar_done", 2)
        crstd_done, cnorm_done = tally("crstd_done", 1), tally("cnorm_done", JT)
        ctr_done, cf_done = tally("ctr_done", JT), tally("cf_done", JT)
        ch_done, cl_done = tally("ch_done", JT), tally("cl_done", JT)
        lat_ready, qproj_done = tally("lat_ready", 1), tally("qproj_done", 1)
        qrow_done, qtr_done = tally("qrow_done", 1), tally("qtr_done", 1)
        qh_done, ql_done = tally("qh_done", 1), tally("ql_done", 1)
        kproj_done, vproj_done = tally("kproj_done", NT), tally("vproj_done", NT)
        kraw_done, rope_done = tally("kraw_done", JT), tally("rope_done", JT)
        krow_done, klat_done = tally("krow_done", JT), tally("klat_done", 1)
        ktr_done, kth_done, ktl_done = tally("ktr_done", NT), tally("kth_done", NT), tally("ktl_done", NT)
        vh_done, vl_done = tally("vh_done", NT), tally("vl_done", NT)
        score_done, max_done, exp_done = tally("score_done", H), tally("max_done", H), tally("exp_done", H)
        inv_done, prob_done = tally("inv_done", H), tally("prob_done", H)
        ptr_done, pth_done, ptl_done = tally("ptr_done", H), tally("pth_done", H), tally("ptl_done", H)
        av_done, oth_done, otl_done = tally("av_done", HP), tally("oth_done", HP), tally("otl_done", HP)
        wo_done, x1_done = tally("wo_done", 1), tally("x1_done", 1)
        ostat_done, oparts_done, ovar_done = tally("ostat_done", 1), tally("oparts_done", 3), tally("ovar_done", 2)
        orstd_done, x2_done = tally("orstd_done", 1), tally("x2_done", 1)

        block = st.enter_context(nc.Block())

        ORDER = [JT, 0, 1, 2]

        def key_bank(n):
            return pk if n == NT - 1 else tp

        LEAD = 6
        VALUES_AT = (2, 4, 6, 8)
        SPLIT_AT = (3, 4, 7, 8)
        PROJECT_AT = (9,)
        OUTPUT_AT = (9, 10, 13)
        END = OUTPUT_AT[-1] + 1

        def due(when, h, this, previous):
            parts = [(n, previous) for n, at in enumerate(when) if at == h + H and previous]
            return parts + [(n, this) for n, at in enumerate(when) if at == h]

        def prepare_beside(prepare, h, half, following, after):
            s = 2 * h + half + LEAD
            if following:
                prepare(*following, s)
            if after and s >= 2 * H:
                prepare(*after, s - 2 * H)

        def frame(eng, prepare, other_latents, begin, head, close):
            for s in range(H + 1):
                prepare(0, 0, 2 * s, first=True)
                prepare(0, 0, 2 * s + 1, first=True)
                other_latents(s)
            begin(0, 0)
            for s in range(LEAD):
                prepare(0, 1, s)

            def batch(t, p, previous, following, after):
                for h in range(H):
                    head(t, p, h, previous, following, after)

            batch(0, 0, None, (0, 1), (1, 0))
            with eng.Fori(0, B // 2 - 2) as t:
                batch(t, 1, (t, 0), (t + 1, 0), (t + 1, 1))
                batch(t + 1, 0, (t, 1), (t + 1, 1), (t + 2, 0))
            t = B // 2 - 1
            batch(t - 1, 1, (t - 1, 0), (t, 0), (t, 1))
            batch(t, 0, (t - 1, 1), (t, 1), None)
            batch(t, 1, (t, 0), None, None)
            close(t, 1)

        def latent_count(r, b1):
            return r + 1 if b1 == 1 else 2 + r * (B - 1) + b1 - 1

        def low_latents(eng, b):
            eng.wait_ge(lnh_done, b + 1)
            eng.tensor_tensor(tokl[:, :, b * M:(b + 1) * M], lf[b % 2],
                              tokh[:, :, b * M:(b + 1) * M].bitcast(F32), ALU.subtract).then_inc(lnl_done, 1)

        def rotate(eng, t, p, j):
            eng.wait_ge(krow_done.sem, krow_done.at(t, p, j))
            eng.wait_ge(kraw_done.sem, kraw_done.at(t, p, j + 1))
            eng.tensor_tensor(kcos.rearrange("q (h c) -> q h c", h=H),
                              krow[:, j].rearrange("q (h c) -> q h c", h=H),
                              rope_t[:, 0, j:j + 1, :].broadcast_to([JR, H, DH]), ALU.mult)
            eng.tensor_tensor(
                ksin.rearrange("q (h s c) -> q h s c", h=H, s=2),
                krow[:, j].rearrange("q (h s c) -> q h s c", h=H, s=2)[:, :, ::-1, :],
                rope_t[:, 1, j:j + 1, :].rearrange("q a (s c) -> q a s c", s=2)
                .broadcast_to([JR, H, 2, DH // 2]), ALU.mult).then_inc(rope_done.sem, 1)
            eng.wait_ge(rope_done.sem, rope_done.at(t, p, j + 1))
            eng.tensor_tensor(krow[:, j], kcos, ksin, ALU.add).then_inc(krow_done.sem, 1)

        LATENTS_AT = {5: (1, 2), 6: (3, 4), 7: (5, 6, 7)}

        @block.sync
        def _(sp):
            sp.dma_start(x_all[:, 0], x[0]).then_inc(x0_loaded, 16)
            for n, v in enumerate((gamma_x, beta_x, gamma_l, beta_l)):
                sp.dma_start(affine_rows[n * KD:(n + 1) * KD, :], v.rearrange("(k p) -> k p", p=P)) \
                    .then_inc(affine_loaded, 16)
            sp.dma_start(w2s[:, 0:4, :].rearrange("p (k a) d -> p k (a d)", k=KD),
                         wq.rearrange("(k p) n -> p k n", p=P)).then_inc(wq_loaded, 16)

            def load_context(t, p):
                sp.wait_ge(ctr_done.sem, ctr_done.at(t, p, -JT))
                sp.dma_start(ctx_t[:, p], ctx[2 * t + p].rearrange("(a r) d -> r a d", a=JT)) \
                    .then_inc(ctx_loaded[p], 16)

            load_context(0, 0)
            sp.dma_start(w1s[:, :, :], wkv.rearrange("(k p) n -> p k n", p=P)).then_inc(wkv_loaded, 16)
            sp.dma_start(x_all[:, 1:B], x[1:B].rearrange("b m d -> m b d")).then_inc(x_loaded, 16)
            load_context(0, 1)
            sp.dma_start(w2s[:, 4:8, :], wo.rearrange("(k p) n -> p k n", p=P)).then_inc(wo_loaded, 16)
            with sp.Fori(1, B // 2) as t:
                load_context(t, 0)
                load_context(t, 1)
            for done in (wkl_done, wvl_done, wql_done, wol_done):
                sp.wait_ge(done, 1)
            sp.dma_start(w1s[:], w1[0].rearrange("(k p) f -> p k f", p=P)).then_inc(w1_loaded, 16)
            sp.dma_start(w2s[:], w2[0].rearrange("(f p) d -> p f d", p=P)).then_inc(w2_loaded, 16)

        @block.gpsimd
        def _(pool):
            for c in (crstd_done, cl_done, rope_done, krow_done, orstd_done, w1l_done, w2l_done):
                c.start(pool)
            pool.memset(ident[:], 0.0).then_inc(const_set, 1)
            pool.memset(neg_half[:], -0.5).then_inc(const_set, 1)
            pool.wait_ge(const_set, 2)
            pool.affine_select(out=ident[:], in_=ident[:], compare_op=ALU.not_equal, fill=1.0, base=0,
                               pattern=[[-1, P]], channel_multiplier=1).then_inc(ident_set, 1)
            pool.dma_start(rope_t[:], rope).then_inc(small_loaded, 16)

            def latent_rstd(r, b0, b1):
                n = latent_count(r, b1)
                pool.wait_ge(lmv_done, n)
                pool.tensor_scalar(lvar[:, b0:b1], lmv[:, b0:b1, 1], EPS, None, ALU.add).then_inc(lvar_done, 1)
                pool.wait_ge(lvar_done, 2 * (b0 > 0) + r + 1)
                pool.tensor_tensor(lrstd[:, b0:b1], lvar[:, b0:b1], neg_half[0:M, b0:b1], ALU.pow) \
                    .then_inc(lrstd_done, 1)

            def other_latents(s):
                if s == 1:
                    pool.wait_ge(whi_done, 3)
                    pool.tensor_tensor(wkvl[:, :, INNER:], w1s[:, :, INNER:], wkvh[:, :, INNER:].bitcast(F32),
                                       ALU.subtract).then_inc(wvl_done, 1)
                    latent_rstd(0, 1, B)
                if s == 3:
                    latent_rstd(1, 1, B)
                if s == H:
                    pool.wait_ge(small_loaded, 4 * 16)
                    pool.wait_ge(wo_loaded, 16)
                    pool.tensor_copy(woh, w2s[:, 4:8, :]).then_inc(woh_done, 1)
                    pool.wait_ge(woh_done, 1)
                    pool.tensor_tensor(wol, w2s[:, 4:8, :], woh.bitcast(F32), ALU.subtract).then_inc(wol_done, 1)

            latent_rstd(0, 0, 1)
            latent_rstd(1, 0, 1)
            for n, g in enumerate((g_xattn, g_ffn)):
                pool.dma_start(gates[:, n:n + 1], g.rearrange("(a b) -> a b", b=1).broadcast_to([P, 1])) \
                    .then_inc(small_loaded, 16)
            low_latents(pool, 0)
            pool.dma_start(wg_t[:], wg.rearrange("(k p) e -> p k e", p=P)).then_inc(small_loaded, 16)

            def low_context(t, p, j):
                pool.wait_ge(ch_done.sem, ch_done.at(t, p, j + 1))
                pool.tensor_tensor(cl[:, j], cf[:, j], ch[:, j].bitcast(F32), ALU.subtract) \
                    .then_inc(cl_done.sem, 1)

            def prepare(t, p, s, first=False):
                if s == 0:
                    pool.wait_ge(cvar_done.sem, cvar_done.at(t, p, 2))
                    pool.tensor_tensor(crstd[:], cvar[:], neg_half[0:JR, 0:JT], ALU.pow).then_inc(crstd_done.sem, 1)
                if s == 4:
                    low_context(t, p, 0)
                if s == 6:
                    low_context(t, p, 1)
                if s == 8:
                    if not first:
                        rotate(pool, t, p, 0)
                if s == 10:
                    low_context(t, p, 2)
                    if not first:
                        rotate(pool, t, p, 1)
                if s == 12:
                    if not first:
                        rotate(pool, t, p, 2)

            def output_rstd(t, p):
                pool.wait_ge(ovar_done.sem, ovar_done.at(t, p, 2))
                pool.tensor_tensor(orstd[:], ovar[:], neg_half[0:M, 0:1], ALU.pow).then_inc(orstd_done.sem, 1)

            def late_rstd(t, p, h, previous):
                for n, batch in due(OUTPUT_AT[1:2], h, (t, p), previous):
                    output_rstd(*batch)

            def head(t, p, h, previous, following, after):
                prepare_beside(prepare, h, 0, following, after)
                prepare_beside(prepare, h, 1, following, after)
                late_rstd(t, p, h, previous)
                if h == 1 and not following:
                    pool.wait_ge(w1h_done.sem, w1h_done.at(0, 0, 1))
                    pool.tensor_tensor(wide[1][:], w1s[:], wide[0][:].bitcast(F32), ALU.subtract) \
                        .then_inc(w1l_done.sem, 1)
                if h == 4 and not following:
                    pool.wait_ge(w2h_done.sem, w2h_done.at(0, 0, 1))
                    pool.tensor_tensor(deep[1][:, 0:4, :], w2s[:, 0:4, :], deep[0][:, 0:4, :].bitcast(F32),
                                       ALU.subtract).then_inc(w2l_done.sem, 1)

            def close(t, p):
                for h in range(H, END):
                    late_rstd(t, p, h, None)

            frame(pool, prepare, other_latents, lambda t, p: None, head, close)

        @block.scalar
        def _(act):
            for c in (lat_ready, qrow_done, cf_done, ch_done, qh_done, kraw_done, klat_done, kth_done,
                      vh_done, exp_done, pth_done, oth_done):
                c.start(act)

            def split_latents(b):
                if b % 2 == 0:
                    act.wait_ge(ltr_done, b + 1)
                    if b >= 2:
                        act.wait_ge(lnl_done, b - 1)
                    for k in range(KD):
                        last = act.activation(lf[0][:, k, :], sc[0][:, k * M:(k + 1) * M], ACT.Identity,
                                              scale=affine[:, 2, k:k + 1], bias=affine[:, 3, k:k + 1])
                    last.then_inc(lf_done[0], 1)
                act.wait_ge(lf_done[b % 2], b // 2 + 1)
                act.copy(tokh[:, :, b * M:(b + 1) * M], lf[b % 2]).then_inc(lnh_done, 1)

            def other_latents(s):
                if s == 0:
                    act.wait_ge(wkv_loaded, 16)
                    for c in (slice(0, INNER), slice(INNER, 2 * INNER)):
                        act.copy(wkvh[:, :, c], w1s[:, :, c]).then_inc(whi_done, 1)
                for b in LATENTS_AT.get(s, ()):
                    split_latents(b)
                if s == 4:
                    act.wait_ge(small_loaded, 4 * 16)
                    act.activation(gates[:], gates[:], ACT.Tanh).then_inc(tanh_done, 1)
                if s == H:
                    act.wait_ge(lnl_done, B)

            act.wait_ge(wq_loaded, 16)
            act.copy(deep[0][:, 0:4, :], w2s[:, 0:4, :]).then_inc(whi_done, 1)
            act.wait_ge(affine_done, 1)
            split_latents(0)
            act.wait_ge(lnl_done, 1)

            def split_context(t, p, j):
                act.wait_ge(ctr_done.sem, ctr_done.at(t, p, j + 1))
                act.wait_ge(cl_done.sem, cl_done.at(t, p, j + 1 - JT))
                for k in range(KD):
                    last = act.activation(cf[:, j, k, :], tp[:, k * JR:(k + 1) * JR], ACT.Identity,
                                          scale=affine[:, 0, k:k + 1], bias=affine[:, 1, k:k + 1])
                last.then_inc(cf_done.sem, 1)
                act.wait_ge(cf_done.sem, cf_done.at(t, p, j + 1))
                act.wait_ge(vproj_done.sem, vproj_done.at(t, p, j + 2 - NT))
                act.copy(ch[:, j], cf[:, j]).then_inc(ch_done.sem, 1)

            def raw_key(t, p, j):
                act.wait_ge(kproj_done.sem, kproj_done.at(t, p, j + 2))
                act.wait_ge(ktr_done.sem, ktr_done.at(t, p, j + 2 - NT))
                act.copy(krow[:, j], pk[0:JR, :]).then_inc(kraw_done.sem, 1)

            def latent_key(t, p):
                act.wait_ge(kproj_done.sem, kproj_done.at(t, p, 1))
                act.wait_ge(qtr_done.sem, qtr_done.at(t, p, 1))
                act.copy(krow[0:M, JT], pk[0:M, :]).then_inc(klat_done.sem, 1)

            def high_value(t, p, n):
                j = ORDER[n]
                rows = M if j == JT else JR
                act.wait_ge(vproj_done.sem, vproj_done.at(t, p, n + 1))
                act.wait_ge(av_done.sem, av_done.at(t, p, -HP))
                act.copy(vh[0:rows, p, j], pv[0:rows, :]).then_inc(vh_done.sem, 1)

            def high_key(t, p, n):
                j = ORDER[n]
                rows = M if j == JT else JR
                act.wait_ge(ktr_done.sem, ktr_done.at(t, p, n + 1))
                act.wait_ge(score_done.sem, score_done.at(t, p, -H))
                act.copy(kth[:, p, :, j * JR:j * JR + rows],
                         key_bank(n)[:, 0:HP * P].rearrange("q (a r) -> q a r", a=HP)[:, :, 0:rows]) \
                    .then_inc(kth_done.sem, 1)

            def prepare(t, p, s, first=False):
                if s == 0:
                    act.wait_ge(vproj_done.sem, vproj_done.at(t, p, -NT))
                    cols = bass.ds((2 * t + p) * M, M)
                    act.copy(lath[:, p], tokh[:, :, cols].bitcast(F32))
                    act.copy(latl[:, p], tokl[:, :, cols].bitcast(F32)).then_inc(lat_ready.sem, 1)
                if s == 2:
                    act.wait_ge(qproj_done.sem, qproj_done.at(t, p, 1))
                    act.wait_ge(ktr_done.sem, ktr_done.at(t, p, 1 - NT))
                    act.mul(qrow, pk[0:M, :], SCALE).then_inc(qrow_done.sem, 1)
                if s == 3:
                    act.wait_ge(qtr_done.sem, qtr_done.at(t, p, 1))
                    act.wait_ge(score_done.sem, score_done.at(t, p, -H))
                    act.copy(qh[:, p], pv[:, 0:HP * M].rearrange("q (a r) -> q a r", a=HP)).then_inc(qh_done.sem, 1)
                if s == 5:
                    split_context(t, p, 0)
                    latent_key(t, p)
                if s == 6:
                    split_context(t, p, 1)
                    high_value(t, p, 0)
                    raw_key(t, p, 0)
                if s == 8:
                    high_value(t, p, 1)
                    high_key(t, p, 0)
                if s == 9:
                    raw_key(t, p, 1)
                if s == 10:
                    split_context(t, p, 2)
                if s == 11:
                    high_value(t, p, 2)
                if s == 12:
                    raw_key(t, p, 2)
                if s == 14:
                    high_value(t, p, 3)
                    high_key(t, p, 1)
                if s == 16:
                    high_key(t, p, 2)
                    high_key(t, p, 3)

            def exponent(t, p, h):
                act.wait_ge(max_done.sem, max_done.at(t, p, h + 1))
                act.wait_ge(ptr_done.sem, ptr_done.at(t, p, h - 1))
                act.activation(prob[:, h % 2, 0:JA], sc[h % 2][0:M, 0:JA], ACT.Exp,
                               bias=negmax[:, h % 2:h % 2 + 1],
                               accum_out=total[:, h % 2:h % 2 + 1]).then_inc(exp_done.sem, 1)

            def high_prob(t, p, h):
                act.wait_ge(ptr_done.sem, ptr_done.at(t, p, h + 1))
                act.wait_ge(av_done.sem, av_done.at(t, p, h // 2 - 1))
                act.copy(pth[:, h // 2 % 2, :, h % 2, :],
                         pt[h % 2][0:JR, 0:NT * M].rearrange("q (a r) -> q a r", a=NT)) \
                    .then_inc(pth_done.sem, 1)

            def high_out(t, p, a):
                act.wait_ge(av_done.sem, av_done.at(t, p, a + 1))
                act.wait_ge(wo_done.sem, wo_done.at(t, p, 0))
                for u in range(2):
                    r = slice(u * DH, (u + 1) * DH)
                    last = act.copy(oth[r, a, :], po[r, u * M:(u + 1) * M])
                last.then_inc(oth_done.sem, 1)

            def begin(t, p):
                exponent(t, p, 0)
                exponent(t, p, 1)

            def late_high_out(t, p, h, previous):
                for n, batch in due(SPLIT_AT, h, (t, p), previous):
                    high_out(*batch, n)

            def head(t, p, h, previous, following, after):
                prepare_beside(prepare, h, 0, following, after)
                high_prob(t, p, h)
                prepare_beside(prepare, h, 1, following, after)
                late_high_out(t, p, h, previous)
                if h + 2 < H:
                    exponent(t, p, h + 2)
                elif following:
                    exponent(*following, h + 2 - H)
                if not following and h < B - 1:
                    high_turned(h)

            def high_turned(b):
                act.wait_ge(turned, b + 1)
                act.copy(tokh[:, :, b * M:(b + 1) * M],
                         tp[:, 0:KD * M].rearrange("q (k m) -> q k m", k=KD)).then_inc(turnh_done, 1)

            def close(t, p):
                for h in range(H, END):
                    late_high_out(t, p, h, None)
                high_turned(B - 1)

            frame(act, prepare, other_latents, begin, head, close)

        @block.vector
        def _(dve):
            for c in (cstat_done, cparts_done, cvar_done, cnorm_done, ql_done, ktl_done, vl_done,
                      max_done, inv_done, prob_done, ptl_done, otl_done, x1_done, ostat_done, oparts_done, ovar_done,
                      x2_done, w1h_done, w2h_done):
                c.start(dve)
            for w in (kth, ktl):
                dve.memset(w[:, :, :, JA:JP].bitcast(F32), 0.0).then_inc(pad_set, 1)
            dve.memset(prob[:, :, JA:PP], 0.0).then_inc(pad_set, 1)

            def latent_stats(r, b0, b1):
                src = x_all if r == 0 else xn
                if r:
                    dve.wait_ge(lnorm_done, latent_count(0, b1))
                for b in range(b0, b1):
                    dve.bn_stats(lstat[:, b, :], src[:, b, :]).then_inc(lstat_done, 1)
                for b in range(b0, b1):
                    dve.wait_ge(lstat_done, latent_count(r, b + 1))
                    dve.bn_aggr(lmv[:, b, :], lstat[:, b, :]).then_inc(lmv_done, 1)

            def latent_norm(r, b0, b1):
                src = x_all if r == 0 else xn
                dve.wait_ge(lmv_done, latent_count(r, b1))
                dve.wait_ge(lrstd_done, 2 * (b0 > 0) + r + 1)
                for b in range(b0, b1):
                    dve.tensor_scalar(xn[:, b, :], src[:, b, :], lmv[:, b, 0:1], lrstd[:, b:b + 1],
                                      ALU.subtract, ALU.mult).then_inc(lnorm_done, 1)

            def affine_latents(b):
                dve.wait_ge(ltr_done, b + 1)
                if b >= 2:
                    dve.wait_ge(lnl_done, b - 1)
                for k in range(KD):
                    last = dve.tensor_scalar(lf[1][:, k, :], sc[1][:, k * M:(k + 1) * M], affine[:, 2, k:k + 1],
                                             affine[:, 3, k:k + 1], ALU.mult, ALU.add)
                last.then_inc(lf_done[1], 1)

            def other_latents(s):
                if s == 1:
                    dve.wait_ge(whi_done, 2)
                    dve.tensor_tensor(wkvl[:, :, 0:INNER], w1s[:, :, 0:INNER], wkvh[:, :, 0:INNER].bitcast(F32),
                                      ALU.subtract).then_inc(wkl_done, 1)
                    dve.wait_ge(x_loaded, 16)
                    latent_stats(0, 1, B)
                if s == 2:
                    latent_norm(0, 1, B)
                if s == 3:
                    latent_stats(1, 1, B)
                if s == 4:
                    latent_norm(1, 1, B)
                for b in LATENTS_AT.get(s, ()):
                    if b % 2:
                        affine_latents(b)
                    low_latents(dve, b)
                if s == 3:
                    dve.wait_ge(small_loaded, 4 * 16)
                if s == 7:
                    dve.tensor_copy(wgh[:], wg_t[:]).then_inc(wg_done, 1)
                    dve.wait_ge(wg_done, 1)
                    dve.tensor_tensor(wgl[:], wg_t[:], wgh[:].bitcast(F32), ALU.subtract).then_inc(wg_done, 1)
                if s == H:
                    dve.wait_ge(tanh_done, 1)

            dve.wait_ge(x0_loaded, 16)
            for r in range(2):
                latent_stats(r, 0, 1)
                latent_norm(r, 0, 1)
            dve.wait_ge(affine_tr, 1)
            dve.tensor_copy(affine[:].rearrange("q n k -> q (n k)"), pt[0][:, 0:4 * KD]).then_inc(affine_done, 1)
            dve.wait_ge(whi_done, 1)
            dve.tensor_tensor(deep[1][:, 0:4, :], w2s[:, 0:4, :], deep[0][:, 0:4, :].bitcast(F32),
                              ALU.subtract).then_inc(wql_done, 1)

            def mean_and_variance(t, p, stat, mean, var, total_, diff, sq, stat_done, parts_done, var_done):
                dve.wait_ge(stat_done.sem, stat_done.at(t, p, stat_done.per))
                dve.tensor_tensor(total_, stat[..., 1], stat[..., 4], ALU.add).then_inc(parts_done.sem, 1)
                dve.tensor_tensor(diff, stat[..., 1], stat[..., 4], ALU.subtract).then_inc(parts_done.sem, 1)
                dve.tensor_tensor(var, stat[..., 2], stat[..., 5], ALU.add)
                dve.wait_ge(parts_done.sem, parts_done.at(t, p, 2))
                dve.tensor_tensor(sq, diff, diff, ALU.mult)
                dve.tensor_scalar(mean, total_, 0.5, None, ALU.mult).then_inc(parts_done.sem, 1)
                dve.wait_ge(parts_done.sem, parts_done.at(t, p, 3))
                dve.scalar_tensor_tensor(var, sq, D / 4.0, var, ALU.mult, ALU.add).then_inc(var_done.sem, 1)
                dve.wait_ge(var_done.sem, var_done.at(t, p, 1))
                dve.tensor_scalar(var, var, 1.0 / D, EPS, ALU.mult, ALU.add).then_inc(var_done.sem, 1)

            def low_value(t, p, n):
                j = ORDER[n]
                rows = M if j == JT else JR
                dve.wait_ge(vh_done.sem, vh_done.at(t, p, n + 1))
                dve.tensor_tensor(vl[0:rows, p, j], pv[0:rows, :], vh[0:rows, p, j].bitcast(F32),
                                  ALU.subtract).then_inc(vl_done.sem, 1)

            def low_key(t, p, n):
                j = ORDER[n]
                rows = M if j == JT else JR
                dve.wait_ge(kth_done.sem, kth_done.at(t, p, n + 1))
                c = slice(j * JR, j * JR + rows)
                dve.tensor_tensor(ktl[:, p, :, c],
                                  key_bank(n)[:, 0:HP * P].rearrange("q (a r) -> q a r", a=HP)[:, :, 0:rows],
                                  kth[:, p, :, c].bitcast(F32), ALU.subtract).then_inc(ktl_done.sem, 1)

            def prepare(t, p, s, first=False):
                if s == 2:
                    dve.wait_ge(ctx_loaded[p], t * 16 + 16)
                    for j in range(JT):
                        dve.bn_stats(cstat[:, j, :], ctx_t[:, p, j, :]).then_inc(cstat_done.sem, 1)
                    mean_and_variance(t, p, cstat[:], cmean[:], cvar[:], csum[:], cdiff[:], csq[:],
                                      cstat_done, cparts_done, cvar_done)
                if s == 3:
                    dve.wait_ge(crstd_done.sem, crstd_done.at(t, p, 1))
                    for j in range(JT):
                        dve.tensor_scalar(ctx_t[:, p, j, :], ctx_t[:, p, j, :], cmean[:, j:j + 1],
                                          crstd[:, j:j + 1], ALU.subtract, ALU.mult).then_inc(cnorm_done.sem, 1)
                if s == 4:
                    dve.wait_ge(qh_done.sem, qh_done.at(t, p, 1))
                    dve.tensor_tensor(ql[:, p], pv[:, 0:HP * M].rearrange("q (a r) -> q a r", a=HP),
                                      qh[:, p].bitcast(F32), ALU.subtract).then_inc(ql_done.sem, 1)
                if s == 6:
                    low_value(t, p, 0)
                if s == 8:
                    low_value(t, p, 1)
                    if first:
                        rotate(dve, t, p, 0)
                    low_key(t, p, 0)
                if s == 11:
                    if first:
                        rotate(dve, t, p, 1)
                if s == 12:
                    low_value(t, p, 2)
                    if first:
                        rotate(dve, t, p, 2)
                if s == 14:
                    low_value(t, p, 3)
                    low_key(t, p, 1)
                if s == 16:
                    low_key(t, p, 2)
                    low_key(t, p, 3)

            def row_max(t, p, h):
                dve.wait_ge(score_done.sem, score_done.at(t, p, h + 1))
                dve.tensor_reduce(negmax[:, h % 2:h % 2 + 1], sc[h % 2][0:M, 0:JA], AX, ALU.max,
                                  negate=True).then_inc(max_done.sem, 1)

            def normalise(t, p, h):
                dve.wait_ge(exp_done.sem, exp_done.at(t, p, h + 1))
                s = slice(h % 2, h % 2 + 1)
                dve.reciprocal(inv[:, s], total[:, s]).then_inc(inv_done.sem, 1)
                dve.wait_ge(inv_done.sem, inv_done.at(t, p, h + 1))
                dve.tensor_scalar(prob[:, h % 2, 0:JA], prob[:, h % 2, 0:JA], inv[:, s], None,
                                  ALU.mult).then_inc(prob_done.sem, 1)

            def low_prob(t, p, h):
                dve.wait_ge(pth_done.sem, pth_done.at(t, p, h + 1))
                s = (slice(None), h // 2 % 2, slice(None), h % 2)
                dve.tensor_tensor(ptl[s], pt[h % 2][0:JR, 0:NT * M].rearrange("q (a r) -> q a r", a=NT),
                                  pth[s].bitcast(F32), ALU.subtract).then_inc(ptl_done.sem, 1)

            def low_out(t, p, a):
                dve.wait_ge(oth_done.sem, oth_done.at(t, p, a + 1))
                for u in range(2):
                    r = slice(u * DH, (u + 1) * DH)
                    last = dve.tensor_tensor(otl[r, a, :], po[r, u * M:(u + 1) * M],
                                             oth[r, a, :].bitcast(F32), ALU.subtract)
                last.then_inc(otl_done.sem, 1)

            def begin(t, p):
                row_max(t, p, 0)
                row_max(t, p, 1)
                normalise(t, p, 0)

            def output(t, p, part):
                row = bass.ds(2 * t + p, 1)
                if part == 0:
                    dve.wait_ge(wo_done.sem, wo_done.at(t, p, 1))
                    dve.scalar_tensor_tensor(x1row[:], po[0:M, 0:D], gates[0:M, 0:1],
                                             x_all[:, row, :].rearrange("q a d -> q (a d)"), ALU.mult, ALU.add) \
                        .then_inc(x1_done.sem, 1)
                if part == 1:
                    dve.wait_ge(x1_done.sem, x1_done.at(t, p, 1))
                    dve.bn_stats(ostat[:], x1row[:]).then_inc(ostat_done.sem, 1)
                    dve.tensor_copy(x_all[:, row, :].rearrange("q a d -> q (a d)"), x1row[:])
                    mean_and_variance(t, p, ostat[:].rearrange("q (a s) -> q a s", a=1), omean[:, 0:1], ovar[:],
                                      omean[:, 1:2], omean[:, 2:3], omean[:, 3:4],
                                      ostat_done, oparts_done, ovar_done)
                if part == 2:
                    dve.wait_ge(orstd_done.sem, orstd_done.at(t, p, 1))
                    dve.tensor_scalar(x2[:, row, :].rearrange("q a d -> q (a d)"), x1row[:],
                                      omean[:, 0:1], orstd[:], ALU.subtract, ALU.mult).then_inc(x2_done.sem, 1)

            def late_low_out(t, p, h, previous):
                for n, batch in due(SPLIT_AT, h, (t, p), previous):
                    low_out(*batch, n)

            def late_output(t, p, h, previous):
                for n, batch in due(OUTPUT_AT, h, (t, p), previous):
                    output(*batch, n)

            def head(t, p, h, previous, following, after):
                if h + 1 < H:
                    normalise(t, p, h + 1)
                elif following:
                    normalise(*following, 0)
                prepare_beside(prepare, h, 0, following, after)
                if h + 2 < H:
                    row_max(t, p, h + 2)
                elif following:
                    row_max(*following, h + 2 - H)
                prepare_beside(prepare, h, 1, following, after)
                low_prob(t, p, h)
                late_low_out(t, p, h, previous)
                late_output(t, p, h, previous)
                if not following:
                    if h == 0:
                        dve.wait_ge(w1_loaded, 16)
                        dve.wait_ge(vproj_done.sem, vproj_done.at(t, p, NT))
                        dve.tensor_copy(wide[0][:], w1s[:]).then_inc(w1h_done.sem, 1)
                    if h == 3:
                        dve.wait_ge(w2_loaded, 16)
                        dve.wait_ge(qproj_done.sem, qproj_done.at(t, p, 1))
                        dve.tensor_copy(deep[0][:, 0:4, :], w2s[:, 0:4, :]).then_inc(w2h_done.sem, 1)
                    if h < B - 1:
                        low_turned(h)

            def low_turned(b):
                dve.wait_ge(turnh_done, b + 1)
                c = slice(b * M, (b + 1) * M)
                dve.tensor_tensor(tokl[:, :, c], tp[:, 0:KD * M].rearrange("q (k m) -> q k m", k=KD),
                                  tokh[:, :, c].bitcast(F32), ALU.subtract).then_inc(turnl_done, 1)

            def close(t, p):
                for h in range(H, END):
                    late_low_out(t, p, h, None)
                    late_output(t, p, h, None)
                low_turned(B - 1)
                dve.wait_ge(logit_done, 1)
                dve.tensor_copy(logit[:], pk[0:M, 0:B * E].rearrange("q (b e) -> q b e", b=B))

            frame(dve, prepare, other_latents, begin, head, close)

        @block.tensor
        def _(pe):
            for c in (ctr_done, qproj_done, qtr_done, kproj_done, vproj_done, ktr_done, score_done,
                      ptr_done, av_done, wo_done):
                c.start(pe)

            def product(dst, terms):
                for n, (ah, al, bh, bl) in enumerate(terms):
                    pe.matmul(dst, ah, bh, start=n == 0, stop=False)
                    pe.matmul(dst, ah, bl, start=False, stop=False)
                    last = pe.matmul(dst, al, bh, start=False, stop=n == len(terms) - 1)
                return last

            pe.wait_ge(ident_set, 1)

            def turn_latents(b):
                pe.wait_ge(lnorm_done, latent_count(1, b + 1))
                if b >= 2:
                    pe.wait_ge(lf_done[b % 2], b // 2)
                for k in range(KD):
                    last = pe.transpose(sc[b % 2][:, k * M:(k + 1) * M], xn[:, b, k * P:(k + 1) * P],
                                        ident[0:M, 0:M])
                last.then_inc(ltr_done, 1)

            def other_latents(s):
                for b in LATENTS_AT.get(s, ()):
                    turn_latents(b)
                if s == H:
                    pe.wait_ge(pad_set, 3)
                    for done in lf_done:
                        pe.wait_ge(done, B // 2)

            pe.wait_ge(affine_loaded, 4 * 16)
            pe.transpose(pt[0][:, 0:4 * KD], affine_rows[:], ident[0:4 * KD, 0:4 * KD]).then_inc(affine_tr, 1)
            turn_latents(0)

            def transpose_context(t, p, j):
                pe.wait_ge(cnorm_done.sem, cnorm_done.at(t, p, j + 1))
                for k in range(KD):
                    last = pe.transpose(tp[:, k * JR:(k + 1) * JR], ctx_t[:, p, j, k * P:(k + 1) * P],
                                        ident[0:JR, 0:JR])
                last.then_inc(ctr_done.sem, 1)

            def rows_of(t, p, n):
                j = ORDER[n]
                return (M, lath[:, p], latl[:, p]) if j == JT else (JR, ch[:, j], cl[:, j])

            def project_keys(t, p, n):
                rows, ah, al = rows_of(t, p, n)
                if n:
                    pe.wait_ge(cl_done.sem, cl_done.at(t, p, n))
                if n == 0:
                    pe.wait_ge(qrow_done.sem, qrow_done.at(t, p, 1))
                    pe.wait_ge(wkl_done, 1)
                elif n == 1:
                    pe.wait_ge(klat_done.sem, klat_done.at(t, p, 1))
                else:
                    pe.wait_ge(kraw_done.sem, kraw_done.at(t, p, n - 1))
                product(pk[0:rows, :], [(ah[:, k], al[:, k], wkvh[:, k, 0:INNER], wkvl[:, k, 0:INNER])
                                        for k in range(KD)]).then_inc(kproj_done.sem, 1)

            def project_values(t, p, n):
                rows, ah, al = rows_of(t, p, n)
                if n == 0:
                    pe.wait_ge(ql_done.sem, ql_done.at(t, p, 1))
                    pe.wait_ge(wvl_done, 1)
                else:
                    pe.wait_ge(vl_done.sem, vl_done.at(t, p, n))
                product(pv[0:rows, :], [(ah[:, k], al[:, k], wkvh[:, k, INNER:], wkvl[:, k, INNER:])
                                        for k in range(KD)]).then_inc(vproj_done.sem, 1)

            def transpose_keys(t, p, n):
                j = ORDER[n]
                rows = M if j == JT else JR
                if j == JT:
                    pe.wait_ge(klat_done.sem, klat_done.at(t, p, 1))
                else:
                    pe.wait_ge(krow_done.sem, krow_done.at(t, p, j + 1))
                for a in range(HP):
                    last = pe.transpose(key_bank(n)[:, a * P:a * P + rows], krow[0:rows, j, a * P:(a + 1) * P],
                                        ident[0:rows, 0:rows])
                last.then_inc(ktr_done.sem, 1)

            def project_queries(t, p):
                pe.wait_ge(lat_ready.sem, lat_ready.at(t, p, 1))
                pe.wait_ge(wql_done, 1)
                pe.wait_ge(ktl_done.sem, ktl_done.at(t, p, 0))
                product(pk[0:M, :], [(lath[:, p, k], latl[:, p, k], wqh[:, k], wql[:, k])
                                     for k in range(KD)]).then_inc(qproj_done.sem, 1)

            def transpose_queries(t, p):
                pe.wait_ge(qrow_done.sem, qrow_done.at(t, p, 1))
                pe.wait_ge(vl_done.sem, vl_done.at(t, p, 0))
                for a in range(HP):
                    last = pe.transpose(pv[:, a * M:(a + 1) * M], qrow[:, a * P:(a + 1) * P], ident[0:M, 0:M])
                last.then_inc(qtr_done.sem, 1)

            def prepare(t, p, s, first=False):
                if s == 0:
                    project_queries(t, p)
                if s == 2:
                    transpose_queries(t, p)
                    transpose_context(t, p, 0)
                if s == 4:
                    project_keys(t, p, 0)
                    pe.wait_ge(cf_done.sem, cf_done.at(t, p, 1))
                    transpose_context(t, p, 1)
                    project_values(t, p, 0)
                if s == 6:
                    project_keys(t, p, 1)
                    pe.wait_ge(cf_done.sem, cf_done.at(t, p, 2))
                    transpose_keys(t, p, 0)
                    project_values(t, p, 1)
                if s == 8:
                    project_keys(t, p, 2)
                    pe.wait_ge(ktl_done.sem, ktl_done.at(t, p, 1))
                    transpose_context(t, p, 2)
                if s == 9:
                    project_values(t, p, 2)
                if s == 11:
                    project_keys(t, p, 3)
                if s == 12:
                    pe.wait_ge(cf_done.sem, cf_done.at(t, p, 3))
                    transpose_keys(t, p, 1)
                    project_values(t, p, 3)
                if s == 14:
                    pe.wait_ge(ktl_done.sem, ktl_done.at(t, p, 2))
                    transpose_keys(t, p, 2)
                    transpose_keys(t, p, 3)

            def scores(t, p, h):
                if h == 0:
                    pe.wait_ge(ktl_done.sem, ktl_done.at(t, p, NT))
                pe.wait_ge(exp_done.sem, exp_done.at(t, p, h - 1))
                r = slice(h % 2 * DH, (h % 2 + 1) * DH)
                a = h // 2
                product(sc[h % 2][0:M, 0:JP], [(qh[r, p, a], ql[r, p, a], kth[r, p, a], ktl[r, p, a])]) \
                    .then_inc(score_done.sem, 1)

            def transpose_probs(t, p, h):
                pe.wait_ge(prob_done.sem, prob_done.at(t, p, h + 1))
                pe.wait_ge(ptl_done.sem, ptl_done.at(t, p, h - 1))
                for j in range(NT):
                    last = pe.transpose(pt[h % 2][0:JR, j * M:(j + 1) * M],
                                        prob[:, h % 2, j * JR:(j + 1) * JR], ident[0:M, 0:M])
                last.then_inc(ptr_done.sem, 1)

            def values(t, p, a):
                pe.wait_ge(ptl_done.sem, ptl_done.at(t, p, 2 * a + 2))
                if a == 0:
                    pe.wait_ge(x1_done.sem, x1_done.at(t, p, 0))
                else:
                    pe.wait_ge(otl_done.sem, otl_done.at(t, p, a))
                c = slice(a * P, (a + 1) * P)
                terms = []
                for j in range(NT):
                    rows = M if j == JT else JR
                    terms.append((vh[0:rows, p, j, c], vl[0:rows, p, j, c],
                                  pth[0:rows, a % 2, j].rearrange("q u m -> q (u m)"),
                                  ptl[0:rows, a % 2, j].rearrange("q u m -> q (u m)")))
                product(po[:, 0:2 * M], terms).then_inc(av_done.sem, 1)

            def begin(t, p):
                scores(t, p, 0)
                scores(t, p, 1)

            def late_values(t, p, h, previous):
                for n, batch in due(VALUES_AT, h, (t, p), previous):
                    values(*batch, n)

            def late_projection(t, p, h, previous):
                for n, batch in due(PROJECT_AT, h, (t, p), previous):
                    project_output(*batch)

            def head(t, p, h, previous, following, after):
                if h < H:
                    transpose_probs(t, p, h)
                if h + 2 < H:
                    scores(t, p, h + 2)
                elif following:
                    scores(*following, h + 2 - H)
                late_values(t, p, h, previous)
                prepare_beside(prepare, h, 0, following, after)
                late_projection(t, p, h, previous)
                prepare_beside(prepare, h, 1, following, after)
                if not following:
                    if h < B - 1:
                        turn(t, p, h)
                    if h:
                        logits(h - 1)

            def turn(t, p, b):
                if b == 0:
                    pe.wait_ge(x2_done.sem, x2_done.at(t, p, -1))
                    pe.wait_ge(ktl_done.sem, ktl_done.at(t, p, NT))
                else:
                    pe.wait_ge(turnl_done, b)
                if b >= B - 2:
                    pe.wait_ge(x2_done.sem, x2_done.at(t, p, b + 2 - B))
                for k in range(KD):
                    last = pe.transpose(tp[:, k * M:(k + 1) * M], x2[:, b, k * P:(k + 1) * P], ident[0:M, 0:M])
                last.then_inc(turned, 1)

            def logits(b):
                pe.wait_ge(turnl_done, b + 1)
                if b == 0:
                    pe.wait_ge(wg_done, 2)
                c = slice(b * M, (b + 1) * M)
                last = product(pk[0:M, b * E:(b + 1) * E],
                               [(tokh[:, k, c], tokl[:, k, c], wgh[:, k, :], wgl[:, k, :]) for k in range(KD)])
                if b == B - 1:
                    last.then_inc(logit_done, 1)

            def close(t, p):
                for h in range(H, END):
                    late_values(t, p, h, None)
                    late_projection(t, p, h, None)
                turn(t, p, B - 1)
                logits(B - 2)
                logits(B - 1)

            def project_output(t, p):
                pe.wait_ge(otl_done.sem, otl_done.at(t, p, HP))
                pe.wait_ge(wol_done, 1)
                product(po[0:M, 0:D], [(oth[:, a], otl[:, a], woh[:, a], wol[:, a]) for a in range(HP)]) \
                    .then_inc(wo_done.sem, 1)

            frame(pe, prepare, other_latents, begin, head, close)


def experts(nc, w1, b1, w2, b2, out, probs_dram, x_all, x2h, x2l, ident, gates, w1s, w2s, wide, deep,
            logit, w1_loaded, w2_loaded, w1h_done, w1l_done, w2h_done, w2l_done):
    with ExitStack() as st:
        def sb(name, shape, dt=F32):
            return st.enter_context(nc.sbuf_tensor(name, shape, dt))

        def sem(name):
            return st.enter_context(nc.semaphore(name))

        def tally(name, per):
            return Tally(sem(name), per)

        be = [M, B, E]
        prob, left, hit, key, first, second, rank = (
            sb(n, be) for n in ("eprob", "left", "hit", "key", "first", "second", "rank"))
        red = sb("red", [M, 8, B])
        pnorm = sb("pnorm", [M, E, B])
        pT = sb("pT", [E * B, M])
        b1rows = sb("b1rows", [E * FB, P])
        b2rows = sb("b2rows", [E, D])
        bT = sb("bT", [P, E * FB + KD * E])
        pb = sb("pb", [P, 2, 2, HALF])
        w1h, w1l = ((w, sb(n, [P, KD, FF], F32R)) for w, n in zip(wide, ("w1h_odd", "w1l_odd")))
        w2h, w2l = ((w, sb(n, [P, FB, D], F32R)) for w, n in zip(deep, ("w2h_odd", "w2l_odd")))
        hf = sb("hf", [P, 2, 2, HALF])
        hh, hl = sb("hh", [P, 2, 2, HALF], F32R), sb("hl", [P, 2, 2, HALF], F32R)
        weighed = sb("weighed", [P, KD * 2, HALF])
        y = sb("y", [P, KD * 2, HALF])
        pu = [st.enter_context(nc.psum_tensor(f"pu{n}", [P, 2, 512], F32)) for n in range(2)]
        py = [st.enter_context(nc.psum_tensor(f"py{n}", [P, 512], F32)) for n in range(4)]

        small_loaded = sem("esmall_loaded")
        router_step, rexp_done, pnorm_done = (sem(n) for n in ("router_step", "rexp_done", "pnorm_done"))
        ptr_done, pT_done, pT_stored, btr_done, bT_done = (
            sem(n) for n in ("eptr_done", "pT_done", "pT_stored", "btr_done", "bT_done"))
        y_set = sem("y_set")
        pb_loaded = [sem("pb_loaded0"), sem("pb_loaded1")]
        up_done, gelu_done, hh_done, hl_done, down_done = (
            tally(n, FB) for n in ("up_done", "gelu_done", "hh_done", "hl_done", "down_done"))
        half_done = tally("half_done", 1)
        weighed_done, added_done = tally("weighed_done", 4), tally("added_done", 1)
        ytr_done, out_done = sem("ytr_done"), sem("out_done")
        summed, stored = sem("summed"), sem("stored")
        rank_set = sem("rank_set")

        GROUPS = (0, 2, 1, 3)

        block = st.enter_context(nc.Block())

        @block.sync
        def _(sp):
            sp.dma_start(b1rows[:], b1.rearrange("e (f p) -> (e f) p", p=P)).then_inc(small_loaded, 16)
            sp.dma_start(b2rows[:], b2).then_inc(small_loaded, 16)
            sp.wait_ge(pT_done, 1)
            sp.dma_start(probs_dram.rearrange("e (b m) -> (e b) m", b=B), pT[:]).then_inc(pT_stored, 16)
            sp.wait_ge(pT_stored, 16)

            def load_weights(t, p, e):
                sp.wait_ge(w1l_done.sem, w1l_done.at(t, p, 0))
                sp.dma_start(w1s[:], w1[e].rearrange("(k p) f -> p k f", p=P)).then_inc(w1_loaded, 16)
                sp.wait_ge(w2l_done.sem, w2l_done.at(t, p, 0))
                sp.dma_start(w2s[:], w2[e].rearrange("(f p) d -> p f d", p=P)).then_inc(w2_loaded, 16)

            def load_probs(t, p, e):
                sp.wait_ge(weighed_done.sem, weighed_done.at(t, p, -4))
                row = probs_dram[e] if isinstance(e, int) else probs_dram[bass.ds(e, 1), :].rearrange("a n -> (a n)")
                sp.dma_start(pb[:, p].rearrange("q a n -> q (a n)"),
                             row.rearrange("(a n) -> a n", a=1).broadcast_to([P, TOK])) \
                    .then_inc(pb_loaded[p], 16)

            load_probs(0, 0, 0)
            load_weights(0, 1, 1)
            load_probs(0, 1, 1)
            with sp.Fori(1, E // 2) as t:
                for p in range(2):
                    load_weights(t, p, 2 * t + p)
                    load_probs(t, p, 2 * t + p)
            for i in range(B // 2):
                sp.wait_ge(out_done, i + 1)
                sp.dma_start(out[2 * i:2 * i + 2].rearrange("b m d -> m b d"), x_all[:, 2 * i:2 * i + 2]) \
                    .then_inc(stored, 16)
            sp.wait_ge(stored, 16 * B // 2)

        @block.gpsimd
        def _(pool):
            added_done.start(pool)
            for e in range(E):
                pool.memset(rank[:, :, e], float(E - e)).then_inc(rank_set, 1)

            def low_weights(t, p, first=False):
                if not first:
                    pool.wait_ge(w1h_done.sem, w1h_done.at(t, p, 1))
                    pool.tensor_tensor(w1l[p][:], w1s[:], w1h[p][:].bitcast(F32), ALU.subtract) \
                        .then_inc(w1l_done.sem, 1)
                for n in range(1 if first else 0, 2):
                    c = slice(n * FB // 2, (n + 1) * FB // 2)
                    pool.wait_ge(w2h_done.sem, w2h_done.at(t, p, n + 1))
                    pool.tensor_tensor(w2l[p][:, c], w2s[:, c], w2h[p][:, c].bitcast(F32), ALU.subtract) \
                        .then_inc(w2l_done.sem, 1)

            def add(t, p):
                pool.wait_ge(weighed_done.sem, weighed_done.at(t, p, 4))
                pool.wait_ge(added_done.sem, added_done.at(t, p, 0))
                pool.tensor_tensor(y[:], y[:], weighed[:], ALU.add).then_inc(added_done.sem, 1)

            low_weights(0, 0, first=True)
            pool.memset(y[:], 0.0).then_inc(y_set, 1)
            pool.wait_ge(y_set, 1)
            with pool.Fori(0, E // 2 - 1) as t:
                low_weights(t, 1)
                add(t, 0)
                low_weights(t + 1, 0)
                add(t, 1)
            low_weights(E // 2 - 1, 1)
            add(E // 2 - 1, 0)

        @block.scalar
        def _(act):
            for c in (gelu_done, hh_done):
                c.start(act)
            act.wait_ge(router_step, 2)
            act.activation(prob[:], left[:], ACT.Exp).then_inc(rexp_done, 1)
            act.copy(w2h[0][:, FB // 2:], w2s[:, FB // 2:]).then_inc(w2h_done.sem, 1)
            act.wait_ge(bT_done, 1)
            with act.Fori(0, E // 2) as t:
                for p in range(2):
                    for f in range(FB):
                        act.wait_ge(up_done.sem, up_done.at(t, p, f + 1))
                        act.wait_ge(hl_done.sem, hl_done.at(t, p, f - 1))
                        act.activation(hf[:, f % 2], pu[f % 2][:, :, 0:HALF], ACT.Gelu,
                                       bias=bT[:, bass.ds(t * (2 * FB) + (p * FB + f), 1)]) \
                            .then_inc(gelu_done.sem, 1)
                        act.wait_ge(gelu_done.sem, gelu_done.at(t, p, f + 1))
                        act.wait_ge(down_done.sem, down_done.at(t, p, f - 1))
                        act.copy(hh[:, f % 2], hf[:, f % 2]).then_inc(hh_done.sem, 1)

        @block.vector
        def _(dve):
            for c in (hl_done, weighed_done):
                c.start(dve)

            def split_high(t, p):
                dve.wait_ge(w1_loaded, t * 32 + 16 * (p + 1))
                dve.wait_ge(up_done.sem, up_done.at(t, p, -FB))
                dve.tensor_copy(w1h[p][:], w1s[:]).then_inc(w1h_done.sem, 1)
                dve.wait_ge(w2_loaded, t * 32 + 16 * (p + 1))
                dve.wait_ge(down_done.sem, down_done.at(t, p, -FB))
                for n in range(2):
                    c = slice(n * FB // 2, (n + 1) * FB // 2)
                    dve.tensor_copy(w2h[p][:, c], w2s[:, c]).then_inc(w2h_done.sem, 1)

            steps = 0

            def step(ins):
                nonlocal steps
                steps += 1
                ins.then_inc(router_step, 1)
                dve.wait_ge(router_step, steps)

            def over_experts(v):
                return v.rearrange("q (b a) -> q b a", a=1).broadcast_to(be)

            step(dve.tensor_reduce(red[:, 0], logit[:], AX, ALU.max))
            step(dve.tensor_tensor(left[:], logit[:], over_experts(red[:, 0]), ALU.subtract))
            dve.wait_ge(btr_done, 1)
            dve.tensor_copy(bT[:], py[2][:, 0:E * FB + KD * E]).then_inc(bT_done, 1)
            dve.wait_ge(rexp_done, 1)
            step(dve.tensor_reduce(red[:, 1], prob[:], AX, ALU.add))
            step(dve.reciprocal(red[:, 2], red[:, 1]))
            step(dve.tensor_tensor(prob[:], prob[:], over_experts(red[:, 2]), ALU.mult))
            dve.wait_ge(rank_set, E)

            def largest(values, onehot, r):
                step(dve.tensor_reduce(red[:, r], values, AX, ALU.max))
                step(dve.tensor_tensor(hit[:], values, over_experts(red[:, r]), ALU.is_equal))
                step(dve.tensor_tensor(key[:], hit[:], rank[:], ALU.mult))
                step(dve.tensor_reduce(red[:, r + 1], key[:], AX, ALU.max))
                step(dve.tensor_tensor(onehot, rank[:], over_experts(red[:, r + 1]), ALU.is_equal))

            largest(prob[:], first[:], 3)
            step(dve.scalar_tensor_tensor(left[:], first[:], -BIG, prob[:], ALU.mult, ALU.add))
            largest(left[:], second[:], 5)
            step(dve.tensor_tensor(hit[:], first[:], second[:], ALU.add))
            step(dve.tensor_tensor(key[:], prob[:], hit[:], ALU.mult))
            step(dve.tensor_reduce(red[:, 0], key[:], AX, ALU.add))
            step(dve.tensor_scalar(red[:, 1], red[:, 0], TOP_EPS, None, ALU.add))
            step(dve.reciprocal(red[:, 2], red[:, 1]))
            dve.tensor_tensor(pnorm[:].rearrange("q e b -> q b e"), key[:], over_experts(red[:, 2]),
                              ALU.mult).then_inc(pnorm_done, 1)

            def low_hidden(t, p, f):
                dve.wait_ge(hh_done.sem, hh_done.at(t, p, f + 1))
                dve.tensor_tensor(hl[:, f % 2], hf[:, f % 2], hh[:, f % 2].bitcast(F32), ALU.subtract) \
                    .then_inc(hl_done.sem, 1)

            def weigh(t, p, g):
                if g == GROUPS[0]:
                    dve.wait_ge(half_done.sem, half_done.at(t, p, 1))
                if g == GROUPS[2]:
                    dve.wait_ge(down_done.sem, down_done.at(t, p, FB))
                col = E * FB + g // 2 * E + p
                dve.scalar_tensor_tensor(weighed[:, g], py[g][:, 0:HALF], bT[:, bass.ds(t * 2 + col, 1)],
                                         pb[:, p, g % 2], ALU.add, ALU.mult).then_inc(weighed_done.sem, 1)

            def last_sum(t):
                for n in range(2):
                    for g in (n, 2 + n):
                        weigh(t, 1, g)
                    for k in range(KD):
                        g = 2 * k + n
                        dve.wait_ge(weighed_done.sem, weighed_done.at(t, 1, 2 * n + k + 1))
                        dve.tensor_tensor(y[:, g], y[:, g], weighed[:, g], ALU.add).then_inc(summed, 1)

            def pair(t, final):
                for p in range(2):
                    for f in range(1, FB + 1):
                        if f < FB:
                            low_hidden(t, p, f)
                        elif p == 0:
                            low_hidden(t, 1, 0)
                        elif not final:
                            low_hidden(t + 1, 0, 0)
                        if f == 4:
                            if p == 0:
                                split_high(t, 1)
                            elif not final:
                                split_high(t + 1, 0)
                    dve.wait_ge(pb_loaded[p], t * 16 + 16)
                    dve.wait_ge(added_done.sem, added_done.at(t, p, 0))
                    if final and p == 1:
                        last_sum(t)
                        continue
                    for g in GROUPS:
                        weigh(t, p, g)

            low_hidden(0, 0, 0)
            dve.wait_ge(ptr_done, 1)
            dve.tensor_copy(pT[:], py[3][0:E * B, 0:M]).then_inc(pT_done, 1)
            with dve.Fori(0, E // 2 - 1) as t:
                pair(t, False)
            pair(E // 2 - 1, True)
            for i in range(B // 2):
                dve.wait_ge(ytr_done, i + 1)
                pair_of = x_all[:, 2 * i:2 * i + 2].rearrange("q b d -> q (b d)")
                dve.scalar_tensor_tensor(pair_of, pu[i // 2][0:M, i % 2, :], gates[0:M, 1:2], pair_of,
                                         ALU.mult, ALU.add).then_inc(out_done, 1)

        @block.tensor
        def _(pe):
            for c in (up_done, down_done, half_done):
                c.start(pe)

            def up(t, p, f):
                if f == 0:
                    pe.wait_ge(w1l_done.sem, w1l_done.at(t, p, 1))
                pe.wait_ge(gelu_done.sem, gelu_done.at(t, p, f - 1))
                c = slice(f * P, (f + 1) * P)
                for n in range(2):
                    s = slice(n * HALF, (n + 1) * HALF)
                    for k in range(KD):
                        pe.matmul(pu[f % 2][:, n, 0:HALF], w1h[p][:, k, c], x2h[:, k, s], start=k == 0, stop=False)
                        pe.matmul(pu[f % 2][:, n, 0:HALF], w1h[p][:, k, c], x2l[:, k, s], start=False, stop=False)
                        last = pe.matmul(pu[f % 2][:, n, 0:HALF], w1l[p][:, k, c], x2h[:, k, s], start=False,
                                         stop=k == KD - 1)
                last.then_inc(up_done.sem, 1)

            def down(t, p, f):
                if f % (FB // 2) == 0:
                    pe.wait_ge(w2l_done.sem, w2l_done.at(t, p, 1 + f // (FB // 2)))
                pe.wait_ge(hl_done.sem, hl_done.at(t, p, f + 1))
                for n, g in enumerate(GROUPS):
                    c = slice(g // 2 * P, (g // 2 + 1) * P)
                    dst = py[g][:, 0:HALF]
                    if f == 0:
                        pe.wait_ge(weighed_done.sem, weighed_done.at(t, p, n + 1 - 4))
                        if g >= 2:
                            pe.wait_ge({2: bT_done, 3: pT_done}[g], 1)
                    pe.matmul(dst, w2h[p][:, f, c], hh[:, f % 2, g % 2], start=f == 0, stop=False)
                    pe.matmul(dst, w2h[p][:, f, c], hl[:, f % 2, g % 2], start=False, stop=False)
                    last = pe.matmul(dst, w2l[p][:, f, c], hh[:, f % 2, g % 2], start=False, stop=f == FB - 1)
                    if f == FB - 1 and n == 1:
                        last.then_inc(half_done.sem, 1)
                last.then_inc(down_done.sem, 1)

            def pair(t, final):
                for p in range(2):
                    for f in range(FB):
                        down(t, p, f)
                        if f + 3 < FB:
                            up(t, p, f + 3)
                        elif p == 0:
                            up(t, 1, f + 3 - FB)
                        elif not final:
                            up(t + 1, 0, f + 3 - FB)

            up(0, 0, 0)
            pe.wait_ge(small_loaded, 32)
            pe.transpose(py[2][:, 0:E * FB], b1rows[:], ident[0:E * FB, 0:E * FB])
            for k in range(KD):
                c = E * FB + k * E
                last = pe.transpose(py[2][:, c:c + E], b2rows[:, k * P:(k + 1) * P], ident[0:E, 0:E])
            last.then_inc(btr_done, 1)
            up(0, 0, 1)
            up(0, 0, 2)
            pe.wait_ge(pnorm_done, 1)
            pe.transpose(py[3][0:E * B, 0:M], pnorm[:].rearrange("q e b -> q (e b)"),
                         ident[0:M, 0:M]).then_inc(ptr_done, 1)
            with pe.Fori(0, E // 2 - 1) as t:
                pair(t, False)
            pair(E // 2 - 1, True)
            pe.wait_ge(gelu_done.sem, gelu_done.at(E // 2 - 1, 1, FB))
            for i in range(B // 2):
                n = i // (B // 4)
                pe.wait_ge(summed, 2 * (n + 1))
                for b in (2 * i, 2 * i + 1):
                    c = b % (B // 2) * M
                    for k in range(KD):
                        last = pe.transpose(pu[i // 2][0:M, i % 2, b % 2 * D + k * P:b % 2 * D + (k + 1) * P],
                                            y[:, 2 * k + n, c:c + M], ident[:, :])
                last.then_inc(ytr_done, 1)


def rope_table(np):
    inv_freq = 1.0 / 10000.0 ** (np.arange(0, DH, 2, dtype=np.float32) / np.float32(DH))
    theta = np.arange(J, dtype=np.float32)[:, None] * inv_freq.astype(np.float32)[None, :]
    cos = np.cos(np.concatenate([theta, theta], axis=1))
    sin = np.sin(np.concatenate([-theta, theta], axis=1))
    t = np.stack([cos, sin]).reshape(2, JT, JR, DH).transpose(2, 0, 1, 3)
    return np.ascontiguousarray(t, dtype=np.float32)


_INS = ["x", "ctx_1024", "g_xattn", "g_ffn", "L0_xattn_gamma_x", "L0_xattn_beta_x", "L0_xattn_gamma_l",
        "L0_xattn_beta_l", "L0_xattn_Wq", "L0_xattn_Wkv", "L0_xattn_Wo", "L0_ffn_Wg", "L0_ffn_W1", "L0_ffn_b1",
        "L0_ffn_W2", "L0_ffn_b2"]


def kernel(**inputs):
    import numpy as np
    from concourse import bacc
    from concourse.bass_utils import run_bass_kernel_spmd

    nc = bacc.Bacc("TRN2", target_bir_lowering=False, num_devices=1)
    arrays = {f"in_{name}": np.ascontiguousarray(inputs[name]) for name in _INS}
    arrays["rope"] = rope_table(np)
    args = [nc.dram_tensor(name, a.shape, mybir.dt.from_np(a.dtype), kind="ExternalInput").ap()
            for name, a in arrays.items()]
    out = nc.dram_tensor("out", (B, M, D), F32, kind="ExternalOutput").ap()
    build_program(nc, *args, out)
    r = run_bass_kernel_spmd(nc, [arrays], core_ids=[0])
    return r.results[0]["out"]
```
